# Optimizing a Trainium2 kernel written in Bass

```python
import numpy as np
import jax
import jax.numpy as jnp

def _softmax(x, axis=-1):
    return jax.nn.softmax(x, axis=axis)

def _gelu(x):
    return jax.nn.gelu(x, approximate=True)

def _silu(x):
    return jax.nn.silu(x)

def _sigmoid(x):
    return jax.nn.sigmoid(x)

def _layernorm(x, axis=-1, eps=1e-05):
    m = jnp.mean(x, axis=axis, keepdims=True)
    v = jnp.var(x, axis=axis, keepdims=True)
    return (x - m) / jnp.sqrt(v + eps)

def _scatter_add(tgt, idx, src, axis=0):
    return tgt.at[idx].add(src)

def _segment_sum(src, seg, n):
    return jax.ops.segment_sum(src, seg, n)
kernel_name = 'mk_flamingo_gated_d1_seqx_r2_f900a3'

def setup_inputs(seed: int=0):
    np.random.seed(seed)
    _w = jnp.asarray

    def _rec_inputs():
        import jax
        import jax.numpy as jnp
        _rk = jax.random.key(seed)
        x = -0.0002928 + 1 * jax.random.normal(jax.random.fold_in(_rk, 1), (8, 512, 512), jnp.float32)
        _lenS = 512 - jax.random.randint(jax.random.fold_in(_rk, 7), (8,), 0, max(1, 512 // 4) + 1, jnp.int32)
        _lenS2 = 512 - jax.random.randint(jax.random.fold_in(_rk, 8), (8,), 0, max(1, 512 // 4) + 1, jnp.int32)
        _ctx_1024P = jax.random.normal(jax.random.fold_in(_rk, 11), (8, 16, 512), jnp.float32)
        _ctx_1024c = jax.random.dirichlet(jax.random.fold_in(_rk, 511), 0.3 * jnp.ones((16,), jnp.float32), (8, 512))
        _ctx_1024t = jnp.einsum('bsk,bkd->bsd', _ctx_1024c, _ctx_1024P)
        _ctx_1024t = _ctx_1024t * jax.lax.rsqrt(jnp.mean(jnp.square(_ctx_1024t)) + 1e-12) * 0.953939
        ctx_1024 = -1.39393e-06 + 0.999914 * (_ctx_1024t + 0.3 * jax.random.normal(jax.random.fold_in(_rk, 611), (8, 512, 512), jnp.float32))
        _g = jax.random.normal(jax.random.fold_in(_rk, 9001), (2, 1), jnp.float32)
        _g = jnp.sign(_g) * jnp.maximum(jnp.abs(_g), 1.0) + (_g == 0) * 1.0
        g_xattn = _g[0]
        g_ffn = _g[1]
        return (x, ctx_1024, g_xattn, g_ffn)
    x, ctx_1024, g_xattn, g_ffn = _rec_inputs()

    def _L0_xattn_setup():
        import jax, jax.numpy as jnp
        import numpy as np
        D_K = 512
        H = 16
        D_H = D_K // H
        key = jax.random.key(seed)
        ks = jax.random.split(key, 11)
        B, S = (2, 1024)
        scale = 1.0 / np.sqrt(D_K)
        inp = {'Q': jax.random.normal(ks[0], (B, S, D_K), jnp.float32), 'K': jax.random.normal(ks[1], (B, S, D_K), jnp.float32), 'V': jax.random.normal(ks[2], (B, S, D_K), jnp.float32), 'Wq': jax.random.normal(ks[3], (D_K, D_K), jnp.float32) * scale, 'bq': jax.random.normal(ks[4], (D_K,), jnp.float32) * 0.01, 'Wk': jax.random.normal(ks[5], (D_K, D_K), jnp.float32) * scale, 'bk': jax.random.normal(ks[6], (D_K,), jnp.float32) * 0.01, 'Wv': jax.random.normal(ks[7], (D_K, D_K), jnp.float32) * scale, 'bv': jax.random.normal(ks[8], (D_K,), jnp.float32) * 0.01, 'Wo': jax.random.normal(ks[9], (D_K, D_K), jnp.float32) * scale, 'bo': jax.random.normal(ks[10], (D_K,), jnp.float32) * 0.01}
        return inp
    _L0_xattn_all = _L0_xattn_setup()
    _L0_xattn_in = {k: v for k, v in _L0_xattn_all.items() if k in ('Wq', 'bq', 'Wk', 'bk', 'Wv', 'bv', 'Wo', 'bo')}
    del _L0_xattn_all

    def _L0_ffn_setup():
        import jax, jax.numpy as jnp
        import numpy as np
        D_MODEL = 512
        DEPTH = 8
        M = 2 ** DEPTH
        N_INTERNAL = M - 1
        B, T = (8, 2048)

        def _leaf_probs(gate):
            BT = gate.shape[0]
            lp = jnp.ones((BT, M), dtype=gate.dtype)
            for level in range(DEPTH):
                n = 2 ** level
                half = M // (2 * n)
                g = gate[:, n - 1:2 * n - 1]
                f = jnp.stack([1.0 - g, g], axis=-1)
                f = jnp.broadcast_to(f[..., None], (BT, n, 2, half))
                lp = lp * f.reshape(BT, M)
            return lp
        key = jax.random.key(seed)
        ks = jax.random.split(key, 7)
        x = jax.random.normal(ks[0], (B, T, D_MODEL), dtype=jnp.float32)
        Wq = jax.random.normal(ks[1], (D_MODEL, D_MODEL), dtype=jnp.float32) * 0.02
        routers = jax.random.normal(ks[2], (N_INTERNAL, D_MODEL), dtype=jnp.float32) * 0.02
        leaf_keys = jax.random.normal(ks[3], (M, D_MODEL), dtype=jnp.float32) * 0.02
        leaf_values = jax.random.normal(ks[4], (M, D_MODEL), dtype=jnp.float32) * 0.02
        Wout_w = jax.random.normal(ks[5], (D_MODEL, D_MODEL), dtype=jnp.float32) * 0.02
        Wout_b = jax.random.normal(ks[6], (D_MODEL,), dtype=jnp.float32) * 0.02
        return {'x': x, 'Wq': Wq, 'routers': routers, 'leaf_keys': leaf_keys, 'leaf_values': leaf_values, 'Wout_w': Wout_w, 'Wout_b': Wout_b}
    _L0_ffn_all = _L0_ffn_setup()
    _L0_ffn_in = {k: v for k, v in _L0_ffn_all.items() if k in ('Wq', 'routers', 'leaf_keys', 'leaf_values', 'Wout_w', 'Wout_b')}
    del _L0_ffn_all
    return {'x': x, 'ctx_1024': ctx_1024, 'g_xattn': g_xattn, 'g_ffn': g_ffn, 'L0_xattn_Wq': _L0_xattn_in['Wq'], 'L0_xattn_bq': _L0_xattn_in['bq'], 'L0_xattn_Wk': _L0_xattn_in['Wk'], 'L0_xattn_bk': _L0_xattn_in['bk'], 'L0_xattn_Wv': _L0_xattn_in['Wv'], 'L0_xattn_bv': _L0_xattn_in['bv'], 'L0_xattn_Wo': _L0_xattn_in['Wo'], 'L0_xattn_bo': _L0_xattn_in['bo'], 'L0_ffn_Wq': _L0_ffn_in['Wq'], 'L0_ffn_routers': _L0_ffn_in['routers'], 'L0_ffn_leaf_keys': _L0_ffn_in['leaf_keys'], 'L0_ffn_leaf_values': _L0_ffn_in['leaf_values'], 'L0_ffn_Wout_w': _L0_ffn_in['Wout_w'], 'L0_ffn_Wout_b': _L0_ffn_in['Wout_b']}

def reference(x, ctx_1024, g_xattn, g_ffn, L0_xattn_Wq, L0_xattn_bq, L0_xattn_Wk, L0_xattn_bk, L0_xattn_Wv, L0_xattn_bv, L0_xattn_Wo, L0_xattn_bo, L0_ffn_Wq, L0_ffn_routers, L0_ffn_leaf_keys, L0_ffn_leaf_values, L0_ffn_Wout_w, L0_ffn_Wout_b):
    import jax
    import jax.numpy as jnp

    def _L0_xattn_ref(Q, K, V, Wq, bq, Wk, bk, Wv, bv, Wo, bo):
        import jax, jax.numpy as jnp
        import numpy as np
        D_K = 512
        H = 16
        D_H = D_K // H
        B, S, _ = Q.shape
        inv_sqrt_dh = 1.0 / np.sqrt(D_H).astype(np.float32)
        q = (Q @ Wq.T + bq).reshape(B, S, H, D_H).transpose(0, 2, 1, 3)
        k = (K @ Wk.T + bk).reshape(B, S, H, D_H).transpose(0, 2, 1, 3)
        v = (V @ Wv.T + bv).reshape(B, S, H, D_H).transpose(0, 2, 1, 3)
        scores = jnp.einsum('bhqd,bhkd->bhqk', q, k) * inv_sqrt_dh
        attn = jax.nn.softmax(scores, axis=-1)
        ctx = jnp.einsum('bhqk,bhkd->bhqd', attn, v)
        ctx = ctx.transpose(0, 2, 1, 3).reshape(B, S, D_K)
        return ctx @ Wo.T + bo

    def _L0_ffn_ref(x, Wq, routers, leaf_keys, leaf_values, Wout_w, Wout_b):
        import jax, jax.numpy as jnp
        import numpy as np
        D_MODEL = 512
        DEPTH = 8
        M = 2 ** DEPTH
        N_INTERNAL = M - 1
        B, T = (8, 2048)

        def _leaf_probs(gate):
            BT = gate.shape[0]
            lp = jnp.ones((BT, M), dtype=gate.dtype)
            for level in range(DEPTH):
                n = 2 ** level
                half = M // (2 * n)
                g = gate[:, n - 1:2 * n - 1]
                f = jnp.stack([1.0 - g, g], axis=-1)
                f = jnp.broadcast_to(f[..., None], (BT, n, 2, half))
                lp = lp * f.reshape(BT, M)
            return lp
        Bv, Tv, d = x.shape
        q = jnp.einsum('btd,ed->bte', x, Wq)
        q_flat = q.reshape(Bv * Tv, d)
        gate = jax.nn.sigmoid(q_flat @ routers.T)
        leaf_prob = _leaf_probs(gate)
        ret = (leaf_prob @ leaf_values).reshape(Bv, Tv, d)
        return jnp.einsum('btd,ed->bte', ret, Wout_w) + Wout_b
    x = x + jnp.tanh(g_xattn[0]) * _L0_xattn_ref(_layernorm(x, axis=-1), ctx_1024, ctx_1024, L0_xattn_Wq, L0_xattn_bq, L0_xattn_Wk, L0_xattn_bk, L0_xattn_Wv, L0_xattn_bv, L0_xattn_Wo, L0_xattn_bo)
    x = x + jnp.tanh(g_ffn[0]) * _L0_ffn_ref(_layernorm(x, axis=-1), L0_ffn_Wq, L0_ffn_routers, L0_ffn_leaf_keys, L0_ffn_leaf_values, L0_ffn_Wout_w, L0_ffn_Wout_b)
    return x

_drawn_inputs = setup_inputs


def setup_inputs(seed=0):
    import zlib

    import numpy as np

    out = dict(_drawn_inputs(seed))
    spreads = {}
    factors = {'L0_xattn_bq': 23.29,
     'L0_xattn_bk': 64.0,
     'L0_xattn_bv': 8.0,
     'L0_xattn_bo': 7.757,
     'L0_ffn_Wq': 8.0,
     'L0_ffn_routers': 8.0,
     'L0_ffn_leaf_values': 8.0,
     'L0_ffn_Wout_w': 8.0,
     'L0_ffn_Wout_b': 3.173}
    for name, (base, spread) in spreads.items():
        noise = np.random.default_rng([zlib.crc32(name.encode()), seed]).standard_normal(out[name].shape)
        drawn = base * np.exp(spread * noise) if base else spread * noise
        out[name] = jnp.asarray(drawn.astype(out[name].dtype))
    for name, factor in factors.items():
        out[name] = (out[name] * factor).astype(out[name].dtype)
    return out
```

```python
from contextlib import ExitStack

import concourse.bass as bass
from concourse import mybir

F32 = mybir.dt.float32
F32R = mybir.dt.float32r
ALU = mybir.AluOpType
ACT = mybir.ActivationFunctionType
AX_X = mybir.AxisListType.X

P = 128
LN_EPS = 1e-5
Z_FLOOR = -40.0


def gated_block(nc, x, ctxT, g_xattn, g_ffn, WqT, bq, WkT, bk, WvT, bv, WoT, bo,
                ffn_Wq, routersT, leaf_valuesT, WoutT, Wout_b, ident_in, out):
    B, S, D = x.shape
    H = 16
    DH = D // H
    KC = D // P
    HG = P // DH
    NT = S // P
    GB = H // HG
    NODES = routersT.shape[1]
    LEAVES = NODES + 1
    LC = LEAVES // P
    DEPTH = LEAVES.bit_length() - 1
    SCALE = float(DH) ** -0.5
    STACK = 3 * DH
    assert KC == HG == NT == GB == 4 and DH == 32

    qT_dram = nc.dram_tensor("qT_split", (B, GB, 2, DH, HG, S), F32).ap()
    kT_dram = nc.dram_tensor("kT_split", (B, GB, 2, DH, HG, S), F32).ap()
    v_dram = nc.dram_tensor("v_by_group", (B, GB, P, NT, P), F32).ap()

    with ExitStack() as ctx:
        def sem(name):
            return ctx.enter_context(nc.semaphore(name))

        def sb(name, shape, dt, stack=ctx):
            return stack.enter_context(nc.sbuf_tensor(name, shape, dt))

        raw = sb("raw", [P, 4, 2048], F32)
        wo = [sb(f"wo_{s}", [P, KC, D], F32R) for s in ("hi", "lo")]
        wz = [sb(f"wz_{s}", [P, KC, LEAVES], F32R) for s in ("hi", "lo")]
        wy = [sb(f"wy_{s}", [P, LC, D], F32R) for s in ("hi", "lo")]
        ident = sb("ident", [P, P], F32)
        ones = sb("ones", [P, DH], F32)
        gates_in = sb("gates_in", [P, 2], F32)
        gain = sb("gain", [P, 2], F32)
        eps = sb("eps", [P, 1], F32)
        g_bo = sb("g_bo", [P, D], F32)
        g_wb = sb("g_wb", [P, D], F32)

        phase0 = ExitStack()
        w_in = {"q": [sb(f"wq_{s}", [P, KC, D], F32R, phase0) for s in ("hi", "lo")]}
        xnT = [sb(f"xnT_{s}", [P, KC, S], F32R, phase0) for s in ("hi", "lo")]
        x_in = sb("x_in", [P, NT, D], F32, phase0)
        xn = sb("xn", [P, NT, D], F32, phase0)
        w_in["k"] = [sb(f"wk_{s}", [P, KC, D], F32R, phase0) for s in ("hi", "lo")]
        c_in = sb("c_in", [P, KC, S], F32, phase0)
        w_in["v"] = [sb(f"wv_{s}", [P, KC, D], F32R, phase0) for s in ("hi", "lo")]
        b_q = sb("b_q", [P, KC], F32, phase0)
        b_k = sb("b_k", [P, KC], F32, phase0)
        b_v = sb("b_v", [P, D], F32, phase0)
        x_stats = sb("x_stats", [P, NT, 6], F32, phase0)
        x_mv = sb("x_mv", [P, NT, 2], F32, phase0)
        x_lnv = sb("x_lnv", [P, NT], F32, phase0)
        x_rstd = sb("x_rstd", [P, NT], F32, phase0)
        cT = [sb(f"cT_{s}", [P, KC, S], F32R, phase0) for s in ("hi", "lo")]
        stage = {n: [sb(f"stage_{n}_{s}", [P, 2, S], F32R, phase0) for s in ("hi", "lo")] for n in "qk"}
        stage_v = sb("stage_v", [P, 2, D], F32, phase0)
        phase0.close()

        q_stack = sb("q_stack", [P, GB, HG, S], F32R)
        k_stack = sb("k_stack", [P, GB, HG, S], F32R)
        v_sb = sb("v_sb", [P, GB, NT, P], F32)
        prob = raw
        pair_sum = sb("pair_sum", [P, 2, HG * S], F32)
        rowmax = sb("rowmax", [P, 2, HG * NT], F32)
        negmax = sb("negmax", [HG * NT, P], F32R)
        inv_den = sb("inv_den", [P, S], F32)
        attn = sb("attn", [P, S], F32)
        aT = [sb(f"aT_{s}", [P, GB, S], F32R) for s in ("hi", "lo")]
        res = sb("res", [P, NT, D], F32)
        r_stats = sb("r_stats", [P, NT, 6], F32)
        r_mv = sb("r_mv", [P, NT, 2], F32)
        r_lnv = sb("r_lnv", [P, NT], F32)
        r_rstd = sb("r_rstd", [P, NT], F32)
        rn = sb("rn", [P, D], F32)
        rnT = [sb(f"rnT_{s}", [P, KC, P], F32R) for s in ("hi", "lo")]
        gate = sb("gate", [P, NT, LEAVES], F32)
        ungate = sb("ungate", [P, NT, LEAVES], F32)
        lp_odd = sb("lp_odd", [P, NT, LEAVES // 2], F32)
        lp = sb("lp", [P, NT, LEAVES], F32)
        lpT = [sb(f"lpT_{s}", [P, LC, P], F32R) for s in ("hi", "lo")]

        bank = [ctx.enter_context(nc.psum_tensor(f"bank{i}", [P, 512], F32)) for i in range(8)]
        bank_a, bank_b, bank_pv, bank_g = bank[0:2], bank[2:4], bank[4:6], bank[6:8]

        w_loaded = [sem(f"w_loaded_{n}") for n in "qkv"]
        small_loaded = sem("small_loaded")
        ffn_w_loaded = sem("ffn_w_loaded")
        consts_set = sem("consts_set")
        raw_cleared = sem("raw_cleared")
        tanh_done = sem("tanh_done")
        w_hi = sem("w_hi")
        w_lo = sem("w_lo")
        x_loaded = sem("x_loaded")
        c_loaded = sem("c_loaded")
        stats_done = sem("stats_done")
        stats_seen = sem("stats_seen")
        mv_done = sem("mv_done")
        lnv_done = sem("lnv_done")
        rstd_done = sem("rstd_done")
        xn_ready = sem("xn_ready")
        xt_done = sem("xt_done")
        xnT_hi_ready = sem("xnT_hi_ready")
        xnT_lo_ready = sem("xnT_lo_ready")
        cT_hi_ready = sem("cT_hi_ready")
        cT_lo_ready = sem("cT_lo_ready")
        proj_done = sem("proj_done")
        proj_hi_staged = sem("proj_hi_staged")
        proj_taken = sem("proj_taken")
        stored = {n: [sem(f"stored_{n}{s}") for s in range(2)] for n in "qkv"}
        prep_done = sem("prep_done")
        prep_hi = sem("prep_hi")
        prep_taken = sem("prep_taken")

        qk_loaded = [sem(f"qk_loaded{c}") for c in range(GB)]
        v_loaded = [sem(f"v_loaded{c}") for c in range(GB)]
        ones_row_set = sem("ones_row_set")
        pass_a_done = sem("pass_a_done")
        max_taken = sem("max_taken")
        max_transposed = sem("max_transposed")
        negmax_ready = sem("negmax_ready")
        maxrow_loaded = sem("maxrow_loaded")
        pass_b_done = sem("pass_b_done")
        exp_done = sem("exp_done")
        pv_done = sem("pv_done")
        pair_ready = sem("pair_ready")
        den_done = sem("den_done")
        lnden_done = sem("lnden_done")
        invden_ready = sem("invden_ready")
        attn_taken = sem("attn_taken")
        aT_hi_ready = sem("aT_hi_ready")
        aT_lo_ready = sem("aT_lo_ready")
        res_loaded = sem("res_loaded")
        res_biased = sem("res_biased")
        o_done = sem("o_done")
        x1_ready = sem("x1_ready")
        r_stats_done = sem("r_stats_done")
        r_mv_done = sem("r_mv_done")
        r_lnv_done = sem("r_lnv_done")
        r_rstd_done = sem("r_rstd_done")
        rn_ready = sem("rn_ready")
        x1_biased = sem("x1_biased")
        rt_done = sem("rt_done")
        rnT_hi_ready = sem("rnT_hi_ready")
        rnT_lo_ready = sem("rnT_lo_ready")
        z_done = sem("z_done")
        z_taken = sem("z_taken")
        sig_step = sem("sig_step")
        gates_ready = sem("gates_ready")
        tree_step = sem("tree_step")
        lt_done = sem("lt_done")
        lpT_hi_ready = sem("lpT_hi_ready")
        lpT_lo_ready = sem("lpT_lo_ready")
        y_done = sem("y_done")
        out_ready = sem("out_ready")
        out_stored = sem("out_stored")

        PROJ_FREE, STAGE_FREE = 6, 32
        RING = 2
        NPROJ = 3 * KC
        TREE_STEPS = DEPTH + 1
        N_PREP = KC + LC

        A_LEAD = 6

        def pass_a_unit(b, c, j, has_next):
            u = HG * c + j + A_LEAD
            if not has_next and u >= HG * GB:
                return None
            return b + u // (HG * GB), u % (HG * GB) // HG, u % HG

        def term_pairs():
            return ((0, 0), (0, 1), (1, 0))

        def stacks_free(eng):
            eng.wait_ge(proj_taken, PROJ_FREE + NPROJ * (B - 1) + 2 * KC)

        def phase0_over(eng):
            eng.wait_ge(proj_taken, PROJ_FREE + NPROJ * B)
            eng.wait_ge(prep_taken, N_PREP)
            eng.wait_ge(cT_lo_ready, KC * B)
            for s in range(2):
                for n in "qkv":
                    per = 16 if n == "v" else 32
                    eng.wait_ge(stored[n][s], STAGE_FREE + per * 2 * B)

        block = ctx.enter_context(nc.Block())

        @block.sync
        def _(sp):
            for n in "qkv":
                for s in range(2):
                    sp.sem_inc(stored[n][s], STAGE_FREE)
            sp.dma_start(x_in[:], x[0].rearrange("(t p) d -> p t d", p=P)).then_inc(x_loaded, 16)
            sp.dma_start(ident[:], ident_in).then_inc(small_loaded, 16)
            sp.dma_start(b_q[:], bq).then_inc(small_loaded, 16)
            sp.dma_start(b_k[:], bk).then_inc(small_loaded, 16)
            sp.dma_start(gates_in[:, 0:1], g_xattn.partition_broadcast(P)).then_inc(small_loaded, 16)
            sp.dma_start(gates_in[:, 1:2], g_ffn.partition_broadcast(P)).then_inc(small_loaded, 16)
            for n, (w, s) in enumerate(((WqT, w_loaded[0]), (WkT, w_loaded[1]), (WvT, w_loaded[2]))):
                sp.dma_start(raw[:, n, :].rearrange("p (k e) -> p k e", k=KC),
                             w.rearrange("(k p) e -> p k e", p=P)).then_inc(s, 16)
                if n == 0:
                    sp.dma_start(c_in[:], ctxT[0].rearrange("(k p) s -> p k s", p=P)).then_inc(c_loaded, 16)
            for dst, src in ((b_v, bv), (g_bo, bo), (g_wb, Wout_b)):
                sp.dma_start(dst[:], src.partition_broadcast(P)).then_inc(small_loaded, 16)
            sp.wait_ge(raw_cleared, 1)
            for dst, src in ((raw[:, 0, :].rearrange("p (k e) -> p k e", k=KC), WoT),
                             (raw[:, 1, :].rearrange("p (k e) -> p k e", k=KC), ffn_Wq),
                             (raw[:, 2, :].rearrange("p (k e) -> p k e", k=KC), WoutT),
                             (raw[:, 3, 0:1024].rearrange("p (k e) -> p k e", k=KC), leaf_valuesT),
                             (raw[:, 3, 1024:2048].rearrange("p (k e) -> p k e", k=KC)[:, :, 0:NODES], routersT)):
                sp.dma_start(dst, src.rearrange("(k p) e -> p k e", p=P)).then_inc(ffn_w_loaded, 16)

            def load_x(b):
                sp.wait_ge(xn_ready, NT * b)
                sp.dma_start(x_in[:], x[b].rearrange("(t p) d -> p t d", p=P)).then_inc(x_loaded, 16)

            def batch(b, has_next, has_second):
                if has_next:
                    sp.wait_ge(cT_lo_ready, KC * b + KC)
                    sp.dma_start(c_in[:], ctxT[b + 1].rearrange("(k p) s -> p k s", p=P)).then_inc(c_loaded, 16)
                for n, dram, first in (("q", qT_dram, 0), ("k", kT_dram, KC)):
                    for c in range(GB):
                        sp.wait_ge(proj_taken, PROJ_FREE + NPROJ * b + first + c + 1)
                        for part in range(2):
                            dst = dram[b, c, part].rearrange("d i s -> i d s")
                            sp.dma_start(dst, stage[n][part][:, c % 2, :].bitcast(F32)).then_inc(stored[n][c % 2], 16)
                    if n == "q" and has_second:
                        load_x(b + 2)
                for t in range(NT):
                    sp.wait_ge(proj_taken, PROJ_FREE + NPROJ * b + 2 * KC + t + 1)
                    sp.dma_start(v_dram[b, :, :, t, :].rearrange("c p e -> p c e"),
                                 stage_v[:, t % 2, :].rearrange("p (c e) -> p c e", c=GB)
                                 ).then_inc(stored["v"][t % 2], 16)

            load_x(1)
            with sp.Fori(0, B - 2) as b:
                batch(b, True, True)
            batch(B - 2, True, False)
            batch(B - 1, False, False)


            def load_group(b, c):
                for r, part in enumerate((0, 0, 1)):
                    sp.dma_start(q_stack[DH * r:DH * (r + 1), c, :, :].bitcast(F32), qT_dram[b, c, part]
                                 ).then_inc(qk_loaded[c], 16)
                for r, part in enumerate((0, 1, 0)):
                    sp.dma_start(k_stack[DH * r:DH * (r + 1), c, :, :].bitcast(F32), kT_dram[b, c, part]
                                 ).then_inc(qk_loaded[c], 16)
                sp.dma_start(v_sb[:, c, :, :], v_dram[b, c]).then_inc(v_loaded[c], 16)

            stacks_free(sp)
            for n in "qk":
                for s in range(2):
                    sp.wait_ge(stored[n][s], STAGE_FREE + 64)
            for s in range(2):
                sp.wait_ge(stored["v"][s], STAGE_FREE + 32)
            for c in range(GB):
                load_group(0, c)
            phase0_over(sp)

            def load_residual(b):
                sp.dma_start(res[:], x[b].rearrange("(t p) d -> p t d", p=P)).then_inc(res_loaded, 16)

            def store_out(b, t):
                sp.wait_ge(out_ready, NT * b + t + 1)
                sp.dma_start(out[b, t * P:(t + 1) * P, :], res[:, t, :]).then_inc(out_stored, 16)

            def iteration(b, has_prev, has_next, second):
                if has_prev:
                    if not second:
                        sp.wait_ge(out_stored, 16 * NT * (b - 1))
                    load_residual(b - 1)
                for c in range(GB):
                    if has_next:
                        sp.wait_ge(pv_done, NT + 16 * b + NT * c + NT)
                        load_group(b + 1, c)
                    if has_prev and c >= 2:
                        store_out(b - 1, 2 * (c - 2))
                        store_out(b - 1, 2 * (c - 2) + 1)

            iteration(0, False, True, False)
            iteration(1, True, True, True)
            with sp.Fori(2, B - 1) as b:
                iteration(b, True, True, False)
            iteration(B - 1, True, False, False)
            sp.wait_ge(out_stored, 16 * NT * (B - 1))
            load_residual(B - 1)
            for t in range(NT):
                store_out(B - 1, t)
            sp.wait_ge(out_stored, 16 * NT * B)

        @block.tensor
        def _(pe):
            def transposes(dst, src_of, n):
                for m in range(n):
                    last = nc.tensor.transpose(dst[:, m * P:(m + 1) * P], src_of(m), ident[:])
                return last

            def split_matmul(dst, left, right, chunks):
                last = None
                for k in range(chunks):
                    for n, (a, m) in enumerate(term_pairs()):
                        last = nc.tensor.matmul(dst, left(a, k), right(m, k), start=(k == 0 and n == 0),
                                                stop=(k == chunks - 1 and n == 2))
                return last

            def transpose_xn(b, k, first=False):
                if not (first and k < 2):
                    pe.wait_ge(xnT_lo_ready, KC * b + k - 1)
                transposes(bank[6 + k % 2], lambda t: xn[:, t, k * P:(k + 1) * P], NT).then_inc(xt_done, 1)

            pe.wait_ge(small_loaded, 16 * 8)
            pe.wait_ge(xn_ready, NT)
            for k in range(KC):
                transpose_xn(0, k, first=True)

            def batch(b, has_next):
                for c in range(KC):
                    pe.wait_ge(proj_taken, NPROJ * b + c + 1)
                    if c == 0:
                        pe.wait_ge(xnT_lo_ready, KC * b + KC)
                    split_matmul(bank[c][:], lambda a, k: w_in["q"][a][:, k, c * P:(c + 1) * P],
                                 lambda m, k: xnT[m][:, k, :], KC).then_inc(proj_done, 1)
                for c in range(KC):
                    pe.wait_ge(proj_taken, NPROJ * b + KC + c + 1)
                    if c == 0:
                        pe.wait_ge(cT_lo_ready, KC * b + KC)
                    split_matmul(bank[(KC + c) % 6][:], lambda a, k: w_in["k"][a][:, k, c * P:(c + 1) * P],
                                 lambda m, k: cT[m][:, k, :], KC).then_inc(proj_done, 1)
                    if has_next:
                        if c == 0:
                            pe.wait_ge(xn_ready, NT * b + 2 * NT)
                        transpose_xn(b + 1, c)
                for t in range(NT):
                    pe.wait_ge(proj_taken, NPROJ * b + 2 * KC + t + 1)
                    split_matmul(bank[(2 * KC + t) % 6][:], lambda a, k: cT[a][:, k, t * P:(t + 1) * P],
                                 lambda m, k: w_in["v"][m][:, k, :], KC).then_inc(proj_done, 1)

            pe.wait_ge(w_lo, 3)
            with pe.Fori(0, B - 1) as b:
                batch(b, True)
            batch(B - 1, False)

            fq = raw[:, 1, :].rearrange("p (k e) -> p k e", k=KC)
            fo = raw[:, 2, :].rearrange("p (k e) -> p k e", k=KC)
            lv = raw[:, 3, 0:1024].rearrange("p (k e) -> p k e", k=KC)
            ro = raw[:, 3, 1024:2048].rearrange("p (k e) -> p k e", k=KC)

            def fold_weights(n):
                dst = bank[6 + n % 2]
                if n >= 2:
                    pe.wait_ge(prep_taken, n - 1)
                for k in range(KC):
                    if n < KC:
                        last = nc.tensor.matmul(dst[:, 0:LEAVES], fq[:, k, n * P:(n + 1) * P], ro[:, k, :],
                                                start=k == 0, stop=k == KC - 1)
                    else:
                        h = n - KC
                        last = nc.tensor.matmul(dst[:], lv[:, k, h * P:(h + 1) * P], fo[:, k, :],
                                                start=k == 0, stop=k == KC - 1)
                last.then_inc(prep_done, 1)

            def score_a(b, c, i, t):
                n = GB * 16 * b + 16 * c + 4 * i + t
                if i == 0 and t == 0:
                    pe.wait_ge(qk_loaded[c], 96 * b + 96)
                pe.wait_ge(max_taken, n + 1)
                nc.tensor.matmul(bank_a[t % 2][:], q_stack[0:STACK, c, i, t * P:(t + 1) * P],
                                 k_stack[0:STACK, c, i, :], start=True, stop=True).then_inc(pass_a_done, 1)

            def score_b(b, c, j, i):
                n = GB * 16 * b + 16 * c + 4 * j + i
                if i == 0 and j == 0:
                    pe.wait_ge(maxrow_loaded, 16 * (GB * b + c + 1))
                pe.wait_ge(exp_done, n + 1)
                nc.tensor.matmul(bank_b[i % 2][:], k_stack[0:STACK + 1, c, i, j * P:(j + 1) * P],
                                 q_stack[0:STACK + 1, c, i, :], start=True, stop=True).then_inc(pass_b_done, 1)

            def prob_v(b, c, j):
                g = GB * b + c
                if j == 0:
                    pe.wait_ge(attn_taken, g + 1)
                    pe.wait_ge(v_loaded[c], 16 * b + 16)
                pe.wait_ge(exp_done, RING + 16 * g + 4 * j + 4)
                for i in range(HG):
                    last = nc.tensor.matmul(bank_pv[c % 2][DH * i:DH * (i + 1), :],
                                            v_sb[:, c, j, DH * i:DH * (i + 1)],
                                            prob[:, j, i * S:(i + 1) * S], start=j == 0, stop=j == NT - 1)
                last.then_inc(pv_done, 1)

            turn = [0]
            readers = [[], []]

            def take_bank(reader):
                s = turn[0]
                turn[0] = 1 - s
                for sema, value in readers[s]:
                    pe.wait_ge(sema, value)
                readers[s] = [reader]
                return bank_g[s]

            def start_turns(known):
                turn[0] = 0
                readers[0], readers[1] = list(known), list(known)

            def transpose_max(b, c):
                g = GB * b + c
                dst = take_bank((negmax_ready, g + 1))
                pe.wait_ge(max_taken, RING + 16 * g + 16)
                nc.tensor.transpose(dst[0:HG * NT, 0:P], rowmax[:, c % 2, :], ident[:]).then_inc(max_transposed, 1)

            def denominators(b, c):
                g = GB * b + c
                dst = take_bank((lnden_done, g + 1))
                pe.wait_ge(pair_ready, 2 + 2 * g + 2)
                for h in range(2):
                    for i in range(HG):
                        last = nc.tensor.matmul(dst[DH * i:DH * (i + 1), :], ones[:], pair_sum[:, h, i * S:(i + 1) * S],
                                                start=h == 0, stop=h == 1)
                last.then_inc(den_done, 1)

            def project_out(b, t):
                dst = take_bank((x1_ready, NT * b + t + 1))
                pe.wait_ge(aT_lo_ready, GB * b + GB)
                split_matmul(dst[:], lambda a, k: aT[a][:, k, t * P:(t + 1) * P],
                             lambda m, k: wo[m][:, k, :], KC).then_inc(o_done, 1)

            def transpose_rn(b, t):
                dst = take_bank((rnT_lo_ready, NT * b + t + 1))
                pe.wait_ge(rn_ready, NT * b + t + 1)
                transposes(dst, lambda k: rn[:, k * P:(k + 1) * P], KC).then_inc(rt_done, 1)

            def route(b, t):
                dst = take_bank((z_taken, NT * b + t + 1))
                pe.wait_ge(rnT_lo_ready, NT * b + t + 1)
                split_matmul(dst[:, 0:LEAVES], lambda a, k: rnT[a][:, k, :],
                             lambda m, k: wz[m][:, k, :], KC).then_inc(z_done, 1)

            def transpose_lp(b, t):
                dst = take_bank((lpT_lo_ready, NT * b + t + 1))
                pe.wait_ge(tree_step, TREE_STEPS * (b + 1))
                transposes(dst, lambda h: lp[:, t, h * P:(h + 1) * P], LC).then_inc(lt_done, 1)

            def leaf_out(b, t):
                dst = take_bank((out_ready, NT * b + t + 1))
                pe.wait_ge(lpT_lo_ready, NT * b + t + 1)
                split_matmul(dst[:], lambda a, k: lpT[a][:, k, :], lambda m, k: wy[m][:, k, :], LC).then_inc(y_done, 1)

            def side_work(b, c, at):
                p = b - 1
                if c == 0:
                    if at == 3:
                        project_out(p, 0)
                        project_out(p, 1)
                    if at == 4:
                        project_out(p, 2)
                        project_out(p, 3)
                if c == 1:
                    if at >= 1:
                        route(p, at - 1)
                    if at <= 3:
                        transpose_rn(p, at)
                if c >= 2 and at <= 3:
                    first, t = (1, 2 * (c - 2)) if c == 2 else (0, 2)
                    if at == first:
                        transpose_lp(p, t)
                    if at == first + 1:
                        leaf_out(p, t)
                        transpose_lp(p, t + 1)
                    if at == first + 2:
                        leaf_out(p, t + 1)

            def group(b, c, has_prev, has_next):
                for j in range(NT):
                    ahead = pass_a_unit(b, c, j, has_next)
                    for half in range(2):
                        for i in (2 * half, 2 * half + 1):
                            score_b(b, c, j, i)
                            if ahead:
                                score_a(*ahead, i)
                        if half == 0 and j:
                            prob_v(b, c, j - 1)
                    if j == 1 and (has_prev or c):
                        if c:
                            denominators(b, c - 1)
                        else:
                            denominators(b - 1, GB - 1)
                    if ahead and ahead[2] == HG - 1:
                        transpose_max(ahead[0], ahead[1])
                    if has_prev:
                        side_work(b, c, j)
                prob_v(b, c, NT - 1)
                if has_prev:
                    side_work(b, c, NT)

            def iteration(b, has_prev, has_next):
                known = [(negmax_ready, GB * b + 1)]
                if has_prev:
                    known.append((lnden_done, GB * (b - 1) + 3))
                    known.append((out_ready, NT * (b - 1)) if not isinstance(b, int) or b > 1 else known[0])
                start_turns(known)
                for c in range(GB):
                    group(b, c, has_prev, has_next)

            pe.wait_ge(proj_taken, PROJ_FREE + NPROJ * B)
            pe.wait_ge(ones_row_set, GB)
            pe.wait_ge(ffn_w_loaded, 16 * 5)
            start_turns([])
            for u in range(A_LEAD):
                for t in range(NT):
                    score_a(0, u // HG, u % HG, t)
                fold_weights(u)
            pe.wait_ge(prep_taken, N_PREP)
            transpose_max(0, 0)
            phase0_over(pe)
            iteration(0, False, True)
            iteration(1, True, True)
            with pe.Fori(2, B - 1) as b:
                iteration(b, True, True)
            iteration(B - 1, True, False)
            denominators(B - 1, GB - 1)
            last = B - 1
            for t in range(NT):
                project_out(last, t)
            for t in range(NT):
                transpose_rn(last, t)
                route(last, t)
            for t in range(NT):
                transpose_lp(last, t)
                leaf_out(last, t)

        @block.scalar
        def _(act):
            act.wait_ge(small_loaded, 16 * 8)
            nc.scalar.activation(gain[:], gates_in[:], ACT.Tanh).then_inc(tanh_done, 1)
            nc.scalar.preload_act_table_set("natural_log_exp_and_others")
            act.wait_ge(consts_set, 2)

            def rstd(b):
                act.wait_ge(mv_done, NT * b + NT)
                nc.scalar.activation(x_lnv[:], x_mv[:, :, 1], ACT.Ln, bias=eps[:]).then_inc(lnv_done, 1)
                act.wait_ge(lnv_done, b + 1)
                nc.scalar.activation(x_rstd[:], x_lnv[:], ACT.Exp, scale=-0.5).then_inc(rstd_done, 1)

            def evac_xt(b, k):
                act.wait_ge(xt_done, KC * b + k + 1)
                nc.scalar.copy(xnT[0][:, k, :], bank[6 + k % 2][:]).then_inc(xnT_hi_ready, 1)

            def evac_proj(b, n, c, first):
                act.wait_ge(proj_done, NPROJ * b + first + c + 1)
                act.wait_ge(stored[n][c % 2], STAGE_FREE + 32 * (2 * b + c // 2))
                nc.scalar.activation(stage[n][0][:, c % 2, :], bank[(first + c) % 6][:], ACT.Identity,
                                     bias=(b_q if n == "q" else b_k)[:, c:c + 1]).then_inc(proj_hi_staged, 1)

            rstd(0)
            for k in range(KC):
                evac_xt(0, k)

            def batch(b, has_next):
                act.wait_ge(c_loaded, 16 * b + 16)
                if not isinstance(b, int) or b:
                    act.wait_ge(proj_done, NPROJ * b)
                for k in range(KC):
                    nc.scalar.copy(cT[0][:, k, :], c_in[:, k, :]).then_inc(cT_hi_ready, 1)
                for c in range(KC):
                    evac_proj(b, "q", c, 0)
                if has_next:
                    rstd(b + 1)
                for c in range(KC):
                    evac_proj(b, "k", c, KC)
                    if has_next:
                        evac_xt(b + 1, c)

            batch(0, True)
            with act.Fori(1, B - 1) as b:
                batch(b, True)
            batch(B - 1, False)

            act.wait_ge(ffn_w_loaded, 16 * 5)
            nc.scalar.copy(wo[0][:].rearrange("p k e -> p (k e)"), raw[:, 0, :]).then_inc(w_hi, 1)
            for n in range(N_PREP):
                act.wait_ge(prep_done, n + 1)
                if n < KC:
                    nc.scalar.copy(wz[0][:, n, :], bank[6 + n % 2][:, 0:LEAVES]).then_inc(prep_hi, 1)
                else:
                    nc.scalar.copy(wy[0][:, n - KC, :], bank[6 + n % 2][:]).then_inc(prep_hi, 1)


            def row_of_maxima(b, c, first=False):
                g = GB * b + c
                act.wait_ge(max_transposed, g + 1)
                if not first:
                    act.wait_ge(maxrow_loaded, 16 * g)
                nc.scalar.mul(negmax[:], bank_max(b, c), -1.0).then_inc(negmax_ready, 1)
                act.wait_ge(negmax_ready, g + 1)
                act.dma_start(q_stack[STACK:STACK + 1, c, :, :].rearrange("o i (t q) -> o (i t) q", q=P).bitcast(F32),
                              negmax[:].bitcast(F32)).then_inc(maxrow_loaded, 16)

            turn = [0]
            where = {}

            def take(kind):
                s = turn[0]
                turn[0] = 1 - s
                where[kind] = bank_g[s]

            def bank_max(b, c):
                return where["max", c][0:HG * NT, 0:P]

            def exp_scores(b, c, j, i):
                g = GB * b + c
                n = 16 * g + 4 * j + i
                act.wait_ge(pass_b_done, n + 1)
                if i == 0:
                    act.wait_ge(pv_done, 4 * g + j + 1)
                    act.wait_ge(pair_ready, 2 * g + j // 2 + 1)
                nc.scalar.activation(prob[:, j, i * S:(i + 1) * S], bank_b[i % 2][:], ACT.Exp,
                                     scale=SCALE).then_inc(exp_done, 1)

            def invert_denominators(b, c):
                g = GB * b + c
                act.wait_ge(den_done, 1 + g + 1)
                act.wait_ge(attn_taken, RING + g)
                nc.scalar.activation(inv_den[:], where["den", c][:], ACT.Ln).then_inc(lnden_done, 1)
                act.wait_ge(lnden_done, g + 1)
                nc.scalar.activation(inv_den[:], inv_den[:], ACT.Exp, scale=-1.0).then_inc(invden_ready, 1)

            def rstd1(b):
                act.wait_ge(r_mv_done, NT * b + NT)
                nc.scalar.activation(r_lnv[:], r_mv[:, :, 1], ACT.Ln, bias=eps[:]).then_inc(r_lnv_done, 1)
                act.wait_ge(r_lnv_done, b + 1)
                nc.scalar.activation(r_rstd[:], r_lnv[:], ACT.Exp, scale=-0.5).then_inc(r_rstd_done, 1)

            def evac_rt(b, t):
                n = NT * b + t
                act.wait_ge(rt_done, n + 1)
                act.wait_ge(z_done, 1 + n)
                nc.scalar.copy(rnT[0][:].rearrange("p k q -> p (k q)"), where["rt", t][:]).then_inc(rnT_hi_ready, 1)

            def sigmoid(b, t):
                n = NT * b + t
                act.wait_ge(z_taken, n + 1)
                nc.scalar.activation(gate[:, t, :], gate[:, t, :], ACT.Exp, scale=-1.0).then_inc(sig_step, 1)
                act.wait_ge(sig_step, 2 * n + 1)
                nc.scalar.activation(gate[:, t, :], gate[:, t, :], ACT.Ln, bias=one_col).then_inc(sig_step, 1)
                act.wait_ge(sig_step, 2 * n + 2)
                nc.scalar.activation(gate[:, t, :], gate[:, t, :], ACT.Exp, scale=-1.0).then_inc(gates_ready, 1)

            def evac_lt(b, t):
                n = NT * b + t
                act.wait_ge(lt_done, n + 1)
                act.wait_ge(y_done, 1 + n)
                nc.scalar.copy(lpT[0][:].rearrange("p k q -> p (k q)"),
                               where["lt", t][:, 0:LC * P]).then_inc(lpT_hi_ready, 1)

            one_col = ones[:, 0:1]

            def side_work(b, c, at):
                p = b - 1
                if c == 0:
                    if at == 3:
                        take("o0"), take("o1")
                    if at == 4:
                        take("o2"), take("o3")
                if c == 1:
                    if at == 0:
                        rstd1(p)
                    if at >= 1:
                        take("z")
                        sigmoid(p, at - 1)
                    if at <= 3:
                        take(("rt", at))
                        evac_rt(p, at)
                if c >= 2 and at <= 3:
                    first, t = (1, 2 * (c - 2)) if c == 2 else (0, 2)
                    if at == first:
                        take(("lt", t))
                        evac_lt(p, t)
                    if at == first + 1:
                        take("y")
                        take(("lt", t + 1))
                        evac_lt(p, t + 1)
                    if at == first + 2:
                        take("y")

            def group(b, c, has_prev, has_next):
                for j in range(NT):
                    ahead = pass_a_unit(b, c, j, has_next)
                    for i in range(HG):
                        exp_scores(b, c, j, i)
                    if j == 1 and (has_prev or c):
                        d = (c - 1) % GB
                        take(("den", d))
                        if c:
                            invert_denominators(b, c - 1)
                        else:
                            invert_denominators(b - 1, GB - 1)
                    if ahead and ahead[2] == HG - 1:
                        take(("max", ahead[1]))
                        row_of_maxima(ahead[0], ahead[1])
                    if has_prev:
                        side_work(b, c, j)
                if has_prev:
                    side_work(b, c, NT)

            def iteration(b, has_prev, has_next):
                turn[0] = 0
                for c in range(GB):
                    group(b, c, has_prev, has_next)

            take(("max", 0))
            row_of_maxima(0, 0, first=True)
            phase0_over(act)
            act.wait_ge(w_lo, 4)
            iteration(0, False, True)
            iteration(1, True, True)
            with act.Fori(2, B - 1) as b:
                iteration(b, True, True)
            iteration(B - 1, True, False)
            last = B - 1
            take(("den", GB - 1))
            invert_denominators(last, GB - 1)
            for t in range(NT):
                take("o")
            rstd1(last)
            for t in range(NT):
                take(("rt", t))
                evac_rt(last, t)
                take("z")
                sigmoid(last, t)
            for t in range(NT):
                take(("lt", t))
                evac_lt(last, t)
                take("y")

        @block.vector
        def _(dve):
            nc.vector.memset(ones[:], 1.0).then_inc(consts_set, 1)
            nc.vector.memset(eps[:], LN_EPS).then_inc(consts_set, 1)
            dve.sem_inc(proj_taken, PROJ_FREE)

            def statistics(b):
                dve.wait_ge(x_loaded, 16 * b + 16)
                for t in range(NT):
                    nc.vector.bn_stats(x_stats[:, t, :], x_in[:, t, :]).then_inc(stats_done, 1)
                dve.wait_ge(stats_done, NT * b + NT)
                dve.sem_inc(stats_seen, 1)
                for t in range(NT):
                    nc.vector.bn_aggr(x_mv[:, t, :], x_stats[:, t, :]).then_inc(mv_done, 1)

            def normalise(b, first=False):
                dve.wait_ge(rstd_done, b + 1)
                if not first:
                    dve.wait_ge(xt_done, KC * b)
                for t in range(NT):
                    nc.vector.tensor_scalar(xn[:, t, :], x_in[:, t, :], x_mv[:, t, 0:1], x_rstd[:, t:t + 1],
                                            ALU.subtract, ALU.mult).then_inc(xn_ready, 1)

            def lo_xt(b, k):
                dve.wait_ge(xnT_hi_ready, KC * b + k + 1)
                nc.vector.tensor_tensor(xnT[1][:, k, :], bank[6 + k % 2][:], xnT[0][:, k, :].bitcast(F32),
                                        ALU.subtract).then_inc(xnT_lo_ready, 1)

            def split_weight(src, dst, hi_count, lo_count):
                nc.vector.tensor_copy(dst[0][:].rearrange("p k e -> p (k e)"), src).then_inc(w_hi, 1)
                dve.wait_ge(w_hi, hi_count)
                return nc.vector.tensor_tensor(dst[1][:].rearrange("p k e -> p (k e)"), src,
                                               dst[0][:].rearrange("p k e -> p (k e)").bitcast(F32),
                                               ALU.subtract).then_inc(w_lo, 1)

            statistics(0)
            normalise(0, first=True)
            for n, name in enumerate("qkv"):
                dve.wait_ge(w_loaded[n], 16)
                split_weight(raw[:, n, :], w_in[name], n + 1, n + 1)
                if n == 0:
                    for k in range(KC):
                        lo_xt(0, k)
            dve.wait_ge(w_lo, 3)
            nc.vector.memset(raw[:, 3, 1024:2048], 0.0).then_inc(raw_cleared, 1)
            dve.wait_ge(small_loaded, 16 * 8)
            dve.wait_ge(tanh_done, 1)
            nc.vector.tensor_scalar(g_bo[:], g_bo[:], gain[:, 0:1], None, ALU.mult).then_inc(consts_set, 1)
            nc.vector.tensor_scalar(g_wb[:], g_wb[:], gain[:, 1:2], None, ALU.mult).then_inc(consts_set, 1)

            def lo_proj(b, n, c, first):
                done = (NPROJ - NT) * b + first + c + 1
                dve.wait_ge(proj_hi_staged, done)
                nc.vector.scalar_tensor_tensor(
                    out=stage[n][1][:, c % 2, :], in0=bank[(first + c) % 6][:],
                    scalar=(b_q if n == "q" else b_k)[:, c:c + 1], in1=stage[n][0][:, c % 2, :].bitcast(F32),
                    op0=ALU.add, op1=ALU.subtract).then_inc(proj_taken, 1)

            def batch(b, has_next):
                for c in range(KC):
                    lo_proj(b, "q", c, 0)
                if has_next:
                    statistics(b + 1)
                    normalise(b + 1)
                for c in range(KC):
                    lo_proj(b, "k", c, KC)
                    if has_next:
                        lo_xt(b + 1, c)
                for t in range(NT):
                    dve.wait_ge(proj_done, NPROJ * b + 2 * KC + t + 1)
                    dve.wait_ge(stored["v"][t % 2], STAGE_FREE + 16 * (2 * b + t // 2))
                    nc.vector.tensor_tensor(stage_v[:, t % 2, :], bank[(2 * KC + t) % 6][:], b_v[:],
                                            ALU.add).then_inc(proj_taken, 1)

            with dve.Fori(0, B - 1) as b:
                batch(b, True)
            batch(B - 1, False)

            dve.sem_inc(max_taken, RING)
            dve.sem_inc(attn_taken, RING)
            dve.wait_ge(w_hi, 4)
            nc.vector.tensor_tensor(wo[1][:].rearrange("p k e -> p (k e)"), raw[:, 0, :],
                                    wo[0][:].rearrange("p k e -> p (k e)").bitcast(F32),
                                    ALU.subtract).then_inc(w_lo, 1)

            def lo_folded(n):
                dve.wait_ge(prep_hi, n + 1)
                if n < KC:
                    hi, lo, src = wz[0][:, n, :], wz[1][:, n, :], bank[6 + n % 2][:, 0:LEAVES]
                else:
                    hi, lo, src = wy[0][:, n - KC, :], wy[1][:, n - KC, :], bank[6 + n % 2][:]
                nc.vector.tensor_tensor(lo, src, hi.bitcast(F32), ALU.subtract).then_inc(prep_taken, 1)

            turn = [0]
            where = {}

            def take(kind):
                s = turn[0]
                turn[0] = 1 - s
                where[kind] = bank_g[s]

            def row_max(b, c, i, t):
                n = GB * 16 * b + 16 * c + 4 * i + t
                dve.wait_ge(pass_a_done, n + 1)
                nc.vector.reduce_max(rowmax[:, c % 2, 4 * i + t:4 * i + t + 1], bank_a[t % 2][:], AX_X
                                     ).then_inc(max_taken, 1)

            def normalise_attn(b, c):
                g = GB * b + c
                dve.wait_ge(invden_ready, g + 1)
                dve.wait_ge(aT_lo_ready, g) if not isinstance(b, int) or g else None
                nc.vector.tensor_tensor(attn[:], bank_pv[c % 2][:], inv_den[:], ALU.mult).then_inc(attn_taken, 1)
                dve.wait_ge(attn_taken, RING + g + 1)
                if not isinstance(b, int) or b:
                    dve.wait_ge(o_done, NT * b)
                nc.vector.tensor_copy(aT[0][:, c, :], attn[:]).then_inc(aT_hi_ready, 1)

            def add_attn(b, t):
                n = NT * b + t
                dve.wait_ge(o_done, n + 1)
                dve.wait_ge(res_biased, n + 1)
                nc.vector.scalar_tensor_tensor(out=res[:, t, :], in0=where["o", t][:], scalar=gain[:, 0:1],
                                               in1=res[:, t, :], op0=ALU.mult, op1=ALU.add).then_inc(x1_ready, 1)
                dve.wait_ge(x1_ready, n + 1)
                nc.vector.bn_stats(r_stats[:, t, :], res[:, t, :]).then_inc(r_stats_done, 1)
                dve.wait_ge(r_stats_done, n + 1)
                dve.sem_inc(stats_seen, 1)
                nc.vector.bn_aggr(r_mv[:, t, :], r_stats[:, t, :]).then_inc(r_mv_done, 1)

            def normalise1(b, t):
                n = NT * b + t
                dve.wait_ge(r_rstd_done, b + 1)
                if not isinstance(b, int) or n:
                    dve.wait_ge(rt_done, n)
                nc.vector.tensor_scalar(rn[:], res[:, t, :], r_mv[:, t, 0:1], r_rstd[:, t:t + 1],
                                        ALU.subtract, ALU.mult).then_inc(rn_ready, 1)

            def lo_rt(b, t):
                dve.wait_ge(rnT_hi_ready, NT * b + t + 1)
                nc.vector.tensor_tensor(rnT[1][:].rearrange("p k q -> p (k q)"), where["rt", t][:],
                                        rnT[0][:].rearrange("p k q -> p (k q)").bitcast(F32),
                                        ALU.subtract).then_inc(rnT_lo_ready, 1)

            def take_z(b, t):
                n = NT * b + t
                dve.wait_ge(z_done, 1 + n + 1)
                nc.vector.tensor_scalar(gate[:, t, :], where["z", t][:, 0:LEAVES], Z_FLOOR, None, ALU.max
                                        ).then_inc(z_taken, 1)

            def leaf_probabilities(b):
                base = TREE_STEPS * b
                dve.wait_ge(gates_ready, NT * b + NT)
                nc.vector.tensor_scalar(ungate[:], gate[:], -1.0, 1.0, ALU.mult, ALU.add).then_inc(tree_step, 1)
                dve.wait_ge(tree_step, base + 1)
                step = 1
                src = None
                for level in range(DEPTH):
                    n = 1 << level
                    dst_t = lp if (DEPTH - 1 - level) % 2 == 0 else lp_odd
                    dst = dst_t[:, :, 0:2 * n].rearrange("p t (m two) -> p t m two", two=2)
                    g1 = gate[:, :, n - 1:2 * n - 1]
                    g0 = ungate[:, :, n - 1:2 * n - 1]
                    if src is None:
                        nc.vector.tensor_copy(dst[:, :, :, 0], g0)
                        last = nc.vector.tensor_copy(dst[:, :, :, 1], g1)
                    else:
                        nc.vector.tensor_tensor(dst[:, :, :, 0], src, g0, ALU.mult)
                        last = nc.vector.tensor_tensor(dst[:, :, :, 1], src, g1, ALU.mult)
                    last.then_inc(tree_step, 1)
                    step += 1
                    dve.wait_ge(tree_step, base + step)
                    src = dst_t[:, :, 0:2 * n]

            def lo_lt(b, t):
                dve.wait_ge(lpT_hi_ready, NT * b + t + 1)
                nc.vector.tensor_tensor(lpT[1][:].rearrange("p k q -> p (k q)"), where["lt", t][:, 0:LC * P],
                                        lpT[0][:].rearrange("p k q -> p (k q)").bitcast(F32),
                                        ALU.subtract).then_inc(lpT_lo_ready, 1)

            def add_ffn(b, t):
                n = NT * b + t
                dve.wait_ge(y_done, 1 + n + 1)
                dve.wait_ge(x1_biased, n + 1)
                nc.vector.scalar_tensor_tensor(out=res[:, t, :], in0=where["y", t][:], scalar=gain[:, 1:2],
                                               in1=res[:, t, :], op0=ALU.mult, op1=ALU.add).then_inc(out_ready, 1)

            def side_work(b, c, at):
                p = b - 1
                if c == 0:
                    if at == 3:
                        take(("o", 0)), take(("o", 1))
                        add_attn(p, 0)
                        add_attn(p, 1)
                    if at == 4:
                        take(("o", 2)), take(("o", 3))
                        add_attn(p, 2)
                        add_attn(p, 3)
                if c == 1:
                    if at >= 1:
                        take(("z", at - 1))
                        take_z(p, at - 1)
                    if at <= 3:
                        take(("rt", at))
                        lo_rt(p, at)
                    if at == 4:
                        leaf_probabilities(p)
                if c >= 2 and at <= 3:
                    first, t = (1, 2 * (c - 2)) if c == 2 else (0, 2)
                    if at == first:
                        take(("lt", t))
                        lo_lt(p, t)
                    if at == first + 1:
                        take(("y", t))
                        add_ffn(p, t)
                        take(("lt", t + 1))
                        lo_lt(p, t + 1)
                    if at == first + 2:
                        take(("y", t + 1))
                        add_ffn(p, t + 1)

            def group(b, c, has_prev, has_next):
                for j in range(NT):
                    ahead = pass_a_unit(b, c, j, has_next)
                    if ahead:
                        for t in range(NT):
                            row_max(*ahead, t)
                    if has_prev and c == 1:
                        normalise1(b - 1, j)
                    if j == 1 and (has_prev or c):
                        take(("den", 0))
                        if c:
                            normalise_attn(b, c - 1)
                        else:
                            normalise_attn(b - 1, GB - 1)
                    if ahead and ahead[2] == HG - 1:
                        take("max")
                    if has_prev:
                        side_work(b, c, j)
                if has_prev:
                    side_work(b, c, NT)

            def iteration(b, has_prev, has_next):
                turn[0] = 0
                for c in range(GB):
                    group(b, c, has_prev, has_next)

            for u in range(A_LEAD):
                for t in range(NT):
                    row_max(0, u // HG, u % HG, t)
                lo_folded(u)
            phase0_over(dve)
            iteration(0, False, True)
            iteration(1, True, True)
            with dve.Fori(2, B - 1) as b:
                iteration(b, True, True)
            iteration(B - 1, True, False)
            last = B - 1
            take(("den", 0))
            normalise_attn(last, GB - 1)
            for t in range(NT):
                take(("o", t))
                add_attn(last, t)
            for t in range(NT):
                normalise1(last, t)
                take(("rt", t))
                lo_rt(last, t)
                take(("z", t))
                take_z(last, t)
            leaf_probabilities(last)
            for t in range(NT):
                take(("lt", t))
                lo_lt(last, t)
                take(("y", t))
                add_ffn(last, t)

        @block.gpsimd
        def _(pool):
            def batch(b):
                for k in range(KC):
                    pool.wait_ge(cT_hi_ready, KC * b + k + 1)
                    nc.gpsimd.tensor_tensor(cT[1][:, k, :], c_in[:, k, :], cT[0][:, k, :].bitcast(F32),
                                            ALU.subtract).then_inc(cT_lo_ready, 1)

            with pool.Fori(0, B) as b:
                batch(b)

            stacks_free(pool)
            for c in range(GB):
                nc.gpsimd.memset(k_stack[STACK:STACK + 1, c, :, :].bitcast(F32), 1.0).then_inc(ones_row_set, 1)
            phase0_over(pool)
            pool.sem_inc(exp_done, RING)
            pool.sem_inc(pv_done, NT)
            pool.sem_inc(pair_ready, 2)
            pool.sem_inc(den_done, 1)
            pool.sem_inc(z_done, 1)
            pool.sem_inc(y_done, 1)

            def add_pair(b, c, h):
                g = GB * b + c
                pool.wait_ge(exp_done, RING + 16 * g + 8 * h + 8)
                pool.wait_ge(den_done, g + 1)
                nc.gpsimd.tensor_tensor(pair_sum[:, h, :], prob[:, 2 * h, :], prob[:, 2 * h + 1, :],
                                        ALU.add).then_inc(pair_ready, 1)

            def lo_attn(b, c):
                pool.wait_ge(aT_hi_ready, GB * b + c + 1)
                nc.gpsimd.tensor_tensor(aT[1][:, c, :], attn[:], aT[0][:, c, :].bitcast(F32),
                                        ALU.subtract).then_inc(aT_lo_ready, 1)

            def bias_residual(b):
                pool.wait_ge(res_loaded, 16 * b + 16)
                for t in range(NT):
                    nc.gpsimd.tensor_tensor(res[:, t, :], res[:, t, :], g_bo[:], ALU.add).then_inc(res_biased, 1)

            def bias_x1(b, t):
                pool.wait_ge(rn_ready, NT * b + t + 1)
                nc.gpsimd.tensor_tensor(res[:, t, :], res[:, t, :], g_wb[:], ALU.add).then_inc(x1_biased, 1)

            def iteration(b, has_prev):
                for c in range(GB):
                    add_pair(b, c, 0)
                    if has_prev or c:
                        if c:
                            lo_attn(b, c - 1)
                        else:
                            lo_attn(b - 1, GB - 1)
                    if has_prev and c == 0:
                        bias_residual(b - 1)
                    add_pair(b, c, 1)
                    if has_prev and c == 1:
                        for t in range(NT):
                            bias_x1(b - 1, t)

            pool.wait_ge(consts_set, 4)
            iteration(0, False)
            with pool.Fori(1, B) as b:
                iteration(b, True)
            lo_attn(B - 1, GB - 1)
            bias_residual(B - 1)
            for t in range(NT):
                bias_x1(B - 1, t)


def kernel(x, ctx_1024, g_xattn, g_ffn, L0_xattn_Wq, L0_xattn_bq, L0_xattn_Wk, L0_xattn_bk, L0_xattn_Wv,
           L0_xattn_bv, L0_xattn_Wo, L0_xattn_bo, L0_ffn_Wq, L0_ffn_routers, L0_ffn_leaf_keys,
           L0_ffn_leaf_values, L0_ffn_Wout_w, L0_ffn_Wout_b):
    import numpy as _np
    import concourse.bacc as _bacc
    from concourse import mybir as _mybir
    from concourse.bass_utils import run_bass_kernel_spmd as _run

    def laid(a):
        return _np.ascontiguousarray(a)

    def columns(v):
        return _np.asarray(v).reshape(-1, 128).T

    given = {
        "x": x,
        "ctxT": _np.asarray(ctx_1024).transpose(0, 2, 1),
        "g_xattn": g_xattn,
        "g_ffn": g_ffn,
        "WqT": _np.asarray(L0_xattn_Wq).T,
        "bq": columns(L0_xattn_bq),
        "WkT": _np.asarray(L0_xattn_Wk).T,
        "bk": columns(L0_xattn_bk),
        "WvT": _np.asarray(L0_xattn_Wv).T,
        "bv": L0_xattn_bv,
        "WoT": _np.asarray(L0_xattn_Wo).T,
        "bo": L0_xattn_bo,
        "ffn_Wq": L0_ffn_Wq,
        "routersT": _np.asarray(L0_ffn_routers).T,
        "leaf_valuesT": _np.asarray(L0_ffn_leaf_values).T,
        "WoutT": _np.asarray(L0_ffn_Wout_w).T,
        "Wout_b": L0_ffn_Wout_b,
        "ident": _np.eye(128, dtype=_np.float32),
    }
    nc = _bacc.Bacc("TRN2", target_bir_lowering=False, num_devices=1)
    arrays, args = {}, []
    for name, a in given.items():
        a = laid(a)
        arrays[f"in_{name}"] = a
        args.append(nc.dram_tensor(f"in_{name}", a.shape, _mybir.dt.from_np(a.dtype), kind="ExternalInput").ap())
    args.append(nc.dram_tensor("out_x", x.shape, _mybir.dt.float32, kind="ExternalOutput").ap())
    gated_block(nc, *args)
    r = _run(nc, [arrays], core_ids=[0])
    return r.results[0]["out_x"]
```

```python
from contextlib import ExitStack

import concourse.bass as bass
from concourse import mybir

F32 = mybir.dt.float32
F32R = mybir.dt.float32r
ALU = mybir.AluOpType
ACT = mybir.ActivationFunctionType
AX_X = mybir.AxisListType.X

P = 128
LN_EPS = 1e-5
Z_FLOOR = -40.0


def gated_block(nc, x, ctxT, g_xattn, g_ffn, WqT, bq, WkT, bk, WvT, bv, WoT, bo,
                ffn_Wq, routersT, leaf_valuesT, WoutT, Wout_b, ident_in, out):
    B, S, D = x.shape
    H = 16
    DH = D // H
    KC = D // P
    HG = P // DH
    NT = S // P
    GB = H // HG
    NODES = routersT.shape[1]
    LEAVES = NODES + 1
    LC = LEAVES // P
    DEPTH = LEAVES.bit_length() - 1
    SCALE = float(DH) ** -0.5
    STACK = 3 * DH
    assert KC == HG == NT == GB == 4 and DH == 32

    qT_dram = nc.dram_tensor("qT_split", (B, GB, 2, DH, HG, S), F32).ap()
    kT_dram = nc.dram_tensor("kT_split", (B, GB, 2, DH, HG, S), F32).ap()
    v_dram = nc.dram_tensor("v_by_group", (B, GB, P, NT, P), F32).ap()

    with ExitStack() as ctx:
        def sem(name):
            return ctx.enter_context(nc.semaphore(name))

        def sb(name, shape, dt, stack=ctx):
            return stack.enter_context(nc.sbuf_tensor(name, shape, dt))

        raw = sb("raw", [P, 4, 2048], F32)
        wo = [sb(f"wo_{s}", [P, KC, D], F32R) for s in ("hi", "lo")]
        wz = [sb(f"wz_{s}", [P, KC, LEAVES], F32R) for s in ("hi", "lo")]
        wy = [sb(f"wy_{s}", [P, LC, D], F32R) for s in ("hi", "lo")]
        ident = sb("ident", [P, P], F32)
        ones = sb("ones", [P, DH], F32)
        gates_in = sb("gates_in", [P, 2], F32)
        gain = sb("gain", [P, 2], F32)
        eps = sb("eps", [P, 1], F32)
        g_bo = sb("g_bo", [P, D], F32)
        g_wb = sb("g_wb", [P, D], F32)

        rowmax = sb("rowmax", [P, 2, HG * NT], F32)
        negmax = sb("negmax", [HG * NT, P], F32R)

        phase0 = ExitStack()
        w_in = {"q": [sb(f"wq_{s}", [P, KC, D], F32R, phase0) for s in ("hi", "lo")]}
        xnT = [sb(f"xnT_{s}", [P, KC, S], F32R, phase0) for s in ("hi", "lo")]
        x_in = sb("x_in", [P, NT, D], F32, phase0)
        xn = sb("xn", [P, NT, D], F32, phase0)
        w_in["k"] = [sb(f"wk_{s}", [P, KC, D], F32R, phase0) for s in ("hi", "lo")]
        c_in = sb("c_in", [P, KC, S], F32, phase0)
        w_in["v"] = [sb(f"wv_{s}", [P, KC, D], F32R, phase0) for s in ("hi", "lo")]
        b_q = sb("b_q", [P, KC], F32, phase0)
        b_k = sb("b_k", [P, KC], F32, phase0)
        b_v = sb("b_v", [P, D], F32, phase0)
        x_stats = sb("x_stats", [P, NT, 6], F32, phase0)
        x_mv = sb("x_mv", [P, NT, 2], F32, phase0)
        x_lnv = sb("x_lnv", [P, NT], F32, phase0)
        x_rstd = sb("x_rstd", [P, NT], F32, phase0)
        cT = [sb(f"cT_{s}", [P, KC, S], F32R, phase0) for s in ("hi", "lo")]
        stage = {n: [sb(f"stage_{n}_{s}", [P, 2, S], F32R, phase0) for s in ("hi", "lo")] for n in "qk"}
        stage_v = sb("stage_v", [P, 2, D], F32, phase0)
        phase0.close()

        q_stack = sb("q_stack", [P, GB, HG, S], F32R)
        k_stack = sb("k_stack", [P, GB, HG, S], F32R)
        v_sb = sb("v_sb", [P, GB, NT, P], F32)
        prob = raw
        pair_sum = sb("pair_sum", [P, 2, HG * S], F32)
        inv_den = sb("inv_den", [P, S], F32)
        attn = sb("attn", [P, S], F32)
        aT = [sb(f"aT_{s}", [P, GB, S], F32R) for s in ("hi", "lo")]
        res = sb("res", [P, NT, D], F32)
        r_stats = sb("r_stats", [P, NT, 6], F32)
        r_mv = sb("r_mv", [P, NT, 2], F32)
        r_lnv = sb("r_lnv", [P, NT], F32)
        r_rstd = sb("r_rstd", [P, NT], F32)
        r_shift = sb("r_shift", [P, NT], F32)
        rn = sb("rn", [P, D], F32)
        rnT = [sb(f"rnT_{s}", [P, KC, P], F32R) for s in ("hi", "lo")]
        gate = sb("gate", [P, NT, LEAVES], F32)
        ungate = sb("ungate", [P, NT, LEAVES], F32)
        lp_odd = sb("lp_odd", [P, NT, LEAVES // 2], F32)
        lp = sb("lp", [P, NT, LEAVES], F32)
        lpT = [sb(f"lpT_{s}", [P, LC, P], F32R) for s in ("hi", "lo")]

        end_rn = pair_sum[:, 0, :].rearrange("p (t d) -> p t d", t=NT)
        end_rnT = [q_stack[:, 0, :, :], q_stack[:, 1, :, :]]
        end_lpT = [q_stack[:, 2, :, :], q_stack[:, 3, :, :]]

        bank = [ctx.enter_context(nc.psum_tensor(f"bank{i}", [P, 512], F32)) for i in range(8)]
        bank_a, bank_b, bank_pv, bank_g = bank[0:2], bank[2:4], bank[4:6], bank[6:8]

        w_loaded = [sem(f"w_loaded_{n}") for n in "qkv"]
        small_loaded = sem("small_loaded")
        ffn_w_loaded = sem("ffn_w_loaded")
        consts_set = sem("consts_set")
        gates_loaded = sem("gates_loaded")
        ident_loaded = sem("ident_loaded")
        raw_cleared = sem("raw_cleared")
        tanh_done = sem("tanh_done")
        w_hi = {n: sem(f"w{n}_hi_ready") for n in "qkvo"}
        w_lo = {n: sem(f"w{n}_lo_ready") for n in "qkvo"}
        x_loaded = sem("x_loaded")
        c_loaded = sem("c_loaded")
        stats_done = sem("stats_done")
        stats_seen = sem("stats_seen")
        mv_done = sem("mv_done")
        lnv_done = sem("lnv_done")
        rstd_done = sem("rstd_done")
        xn_ready = sem("xn_ready")
        xt_done = sem("xt_done")
        xnT_hi_ready = sem("xnT_hi_ready")
        xnT_lo_ready = sem("xnT_lo_ready")
        cT_hi_ready = sem("cT_hi_ready")
        cT_lo_ready = sem("cT_lo_ready")
        proj_done = sem("proj_done")
        proj_hi_staged = sem("proj_hi_staged")
        proj_taken = sem("proj_taken")
        stored = {n: [sem(f"stored_{n}{s}") for s in range(2)] for n in "qkv"}
        prep_done = sem("prep_done")
        prep_hi = sem("prep_hi")
        prep_taken = sem("prep_taken")

        qk_loaded = [sem(f"qk_loaded{c}") for c in range(GB)]
        v_loaded = [sem(f"v_loaded{c}") for c in range(GB)]
        ones_row_set = sem("ones_row_set")
        pass_a_done = sem("pass_a_done")
        max_taken = sem("max_taken")
        max_transposed = sem("max_transposed")
        negmax_ready = sem("negmax_ready")
        maxrow_loaded = sem("maxrow_loaded")
        pass_b_done = sem("pass_b_done")
        exp_done = sem("exp_done")
        pv_done = sem("pv_done")
        pair_ready = sem("pair_ready")
        den_done = sem("den_done")
        lnden_done = sem("lnden_done")
        invden_ready = sem("invden_ready")
        attn_taken = sem("attn_taken")
        aT_hi_ready = sem("aT_hi_ready")
        aT_lo_ready = sem("aT_lo_ready")
        res_loaded = [sem(f"res_loaded{t}") for t in range(NT)]
        res_biased = sem("res_biased")
        o_done = sem("o_done")
        x1_ready = sem("x1_ready")
        r_stats_done = sem("r_stats_done")
        r_mv_done = sem("r_mv_done")
        r_lnv_done = sem("r_lnv_done")
        r_rstd_done = sem("r_rstd_done")
        r_shift_done = sem("r_shift_done")
        rn_ready = sem("rn_ready")
        x1_biased = sem("x1_biased")
        rt_done = sem("rt_done")
        rnT_hi_ready = sem("rnT_hi_ready")
        rnT_lo_ready = sem("rnT_lo_ready")
        z_done = sem("z_done")
        z_taken = sem("z_taken")
        sig_step = sem("sig_step")
        gates_ready = sem("gates_ready")
        tree_step = sem("tree_step")
        lt_done = sem("lt_done")
        lpT_hi_ready = sem("lpT_hi_ready")
        lpT_lo_ready = sem("lpT_lo_ready")
        y_done = sem("y_done")
        out_ready = sem("out_ready")
        out_stored = [sem(f"out_stored{t}") for t in range(NT)]

        PROJ_FREE, STAGE_FREE = 6, 32
        RING = 2
        NPROJ = 3 * KC
        PAIRS = NT // 2
        TREE_STEPS = PAIRS * DEPTH
        N_PREP = KC + LC

        A_LEAD = 7
        TICKS = GB * NT

        SIDE = {
            0: [("lt", 2, 0)],
            1: [("max", 0, 0), ("y", 2, 0), ("lt", 2, 1)],
            2: [("den", 0, 0), ("y", 2, 1), ("lt", 2, 2)],
            3: [("y", 2, 2), ("lt", 2, 3)],
            4: [("y", 2, 3), ("o", 1, 0)],
            5: [("max", 0, 1), ("o", 1, 1)],
            6: [("den", 0, 1), ("o", 1, 2)],
            7: [("o", 1, 3)],
            9: [("max", 0, 2)],
            10: [("den", 0, 2), ("rt", 1, 0)],
            11: [("z", 1, 0), ("rt", 1, 1)],
            12: [("z", 1, 1), ("rt", 1, 2)],
            13: [("max", 0, 3), ("z", 1, 2), ("rt", 1, 3)],
            14: [("den", 0, 3), ("z", 1, 3)],
        }
        RSTD_TICK, RN_TICK = 9, 10
        SIGMOID_AT = {(13, 3): (1, 0, 0), (14, 0): (1, 0, 1), (14, 1): (1, 0, 2), (14, 2): (1, 0, 3),
                      (15, 2): (1, 1, 0), (15, 3): (1, 1, 1), (0, 0): (2, 1, 2), (0, 1): (2, 1, 3)}
        TREE_AT = {(15, 0): (1, 0, (0, 1)), (15, 1): (1, 0, (2, 3)), (15, 2): (1, 0, (4, 5)), (15, 3): (1, 0, (6, 7)),
                   (0, 2): (2, 1, (0, 1, 2, 3)), (0, 3): (2, 1, (4, 5)), (1, 2): (2, 1, (6,)), (1, 3): (2, 1, (7,))}

        def side_at(tick, back, has_next):
            found = []
            for kind, ago, n in SIDE.get(tick, []):
                if kind == "max" and n == GB - 1 and not has_next:
                    continue
                if kind == "den" and n == 0 and not back:
                    continue
                if ago <= back:
                    found.append((kind, ago, n))
            return found

        class Turns:

            def __init__(self):
                self.next = 0
                self.where = {}

            def take(self, kind, tile=0):
                self.where[kind, tile] = bank_g[self.next]
                self.next = 1 - self.next
                return self.where[kind, tile]

        def pass_a_unit(b, c, j, has_next):
            u = HG * c + j + A_LEAD
            if not has_next and u >= HG * GB:
                return None
            return b + u // (HG * GB), u % (HG * GB) // HG, u % HG

        def term_pairs():
            return ((0, 0), (0, 1), (1, 0))

        def stacks_free(eng):
            eng.wait_ge(proj_taken, PROJ_FREE + NPROJ * (B - 1) + 2 * KC)

        def phase0_over(eng):
            eng.wait_ge(proj_taken, PROJ_FREE + NPROJ * B)
            eng.wait_ge(prep_taken, N_PREP)
            eng.wait_ge(cT_lo_ready, KC * B)
            for s in range(2):
                for n in "qkv":
                    per = 16 if n == "v" else 32
                    eng.wait_ge(stored[n][s], STAGE_FREE + per * 2 * B)

        block = ctx.enter_context(nc.Block())

        @block.sync
        def _(sp):
            for n in "qkv":
                for s in range(2):
                    sp.sem_inc(stored[n][s], STAGE_FREE)
            for n, g in enumerate((g_xattn, g_ffn)):
                sp.dma_start(gates_in[:, n:n + 1], g.partition_broadcast(P)).then_inc(gates_loaded, 16)
            sp.dma_start(x_in[:], x[0].rearrange("(t p) d -> p t d", p=P)).then_inc(x_loaded, 16)
            sp.dma_start(ident[:], ident_in).then_inc(ident_loaded, 16)
            for n, (w, s) in enumerate(((WqT, w_loaded[0]), (WkT, w_loaded[1]), (WvT, w_loaded[2]))):
                sp.dma_start(raw[:, n, :].rearrange("p (k e) -> p k e", k=KC),
                             w.rearrange("(k p) e -> p k e", p=P)).then_inc(s, 16)
                if n == 0:
                    sp.dma_start(c_in[:], ctxT[0].rearrange("(k p) s -> p k s", p=P)).then_inc(c_loaded, 16)
            sp.dma_start(b_q[:], bq).then_inc(small_loaded, 16)
            sp.dma_start(b_k[:], bk).then_inc(small_loaded, 16)
            for dst, src in ((b_v, bv), (g_bo, bo), (g_wb, Wout_b)):
                sp.dma_start(dst[:], src.partition_broadcast(P)).then_inc(small_loaded, 16)
            def load_stacks(b, c, which="qk"):
                for n, stack, dram, parts in (("q", q_stack, qT_dram, (0, 0, 1)), ("k", k_stack, kT_dram, (0, 1, 0))):
                    if n in which:
                        for r, part in enumerate(parts):
                            sp.dma_start(stack[DH * r:DH * (r + 1), c, :, :].bitcast(F32), dram[b, c, part]
                                         ).then_inc(qk_loaded[c], 16)

            def load_v(b, c):
                sp.dma_start(v_sb[:, c, :, :], v_dram[b, c]).then_inc(v_loaded[c], 16)

            def load_x(b):
                sp.wait_ge(xn_ready, NT * b)
                sp.dma_start(x_in[:], x[b].rearrange("(t p) d -> p t d", p=P)).then_inc(x_loaded, 16)

            def batch(b, has_next, has_second):
                if has_next:
                    sp.wait_ge(cT_lo_ready, KC * b + KC)
                    sp.dma_start(c_in[:], ctxT[b + 1].rearrange("(k p) s -> p k s", p=P)).then_inc(c_loaded, 16)
                for n, dram, first in (("q", qT_dram, 0), ("k", kT_dram, KC)):
                    for c in range(GB):
                        sp.wait_ge(proj_taken, PROJ_FREE + NPROJ * b + first + c + 1)
                        for part in range(2):
                            dst = dram[b, c, part].rearrange("d i s -> i d s")
                            sp.dma_start(dst, stage[n][part][:, c % 2, :].bitcast(F32)).then_inc(stored[n][c % 2], 16)
                    if n == "q" and has_second:
                        load_x(b + 2)
                    if n == "q" and not has_next:
                        for s in range(2):
                            for m in "qk":
                                sp.wait_ge(stored[m][s], STAGE_FREE + 64)
                            sp.wait_ge(stored["v"][s], STAGE_FREE + 32)
                        for g in range(2):
                            load_stacks(0, g, "q")
                if not has_next:
                    stacks_free(sp)
                    for g in range(2):
                        load_stacks(0, g, "k")
                for t in range(NT):
                    sp.wait_ge(proj_taken, PROJ_FREE + NPROJ * b + 2 * KC + t + 1)
                    sp.dma_start(v_dram[b, :, :, t, :].rearrange("c p e -> p c e"),
                                 stage_v[:, t % 2, :].rearrange("p (c e) -> p c e", c=GB)
                                 ).then_inc(stored["v"][t % 2], 16)

            load_x(1)
            batch(0, True, True)
            def load_weight(w, dst):
                sp.dma_start(dst.rearrange("p (k e) -> p k e", k=KC)[:, :, 0:w.shape[1]],
                             w.rearrange("(k p) e -> p k e", p=P)).then_inc(ffn_w_loaded, 16)

            sp.wait_ge(raw_cleared, 1)
            load_weight(WoT, raw[:, 0, :])
            with sp.Fori(1, B - 3) as b:
                batch(b, True, True)
            load_weight(ffn_Wq, raw[:, 1, :])
            batch(B - 3, True, True)
            load_weight(WoutT, raw[:, 2, :])
            batch(B - 2, True, False)
            load_weight(leaf_valuesT, raw[:, 3, 0:1024])
            load_weight(routersT, raw[:, 3, 1024:2048])
            batch(B - 1, False, False)


            sp.wait_ge(cT_lo_ready, KC * B)
            for c in range(GB):
                if c >= 2:
                    load_stacks(0, c)
                load_v(0, c)
            phase0_over(sp)

            def store_out(b, t):
                sp.wait_ge(out_ready, NT * b + t + 1)
                sp.dma_start(out[b, t * P:(t + 1) * P, :], res[:, t, :]).then_inc(out_stored[t], 16)

            def load_residual(b, t, first=False):
                if not first:
                    sp.wait_ge(out_stored[t], 16 * b)
                sp.dma_start(res[:, t, :], x[b, t * P:(t + 1) * P, :]).then_inc(res_loaded[t], 16)

            def next_group(b, c):
                sp.wait_ge(pv_done, NT + 16 * b + NT * c + NT)
                load_stacks(b + 1, c)
                load_v(b + 1, c)

            def iteration(b, back, has_next):
                for t in range(NT):
                    if back >= 2:
                        store_out(b - 2, t)
                    if back >= 1:
                        load_residual(b - 1, t, first=back == 1)
                    if t == 2 and has_next:
                        next_group(b, 0)
                if has_next:
                    for c in range(1, GB):
                        next_group(b, c)

            iteration(0, 0, True)
            iteration(1, 1, True)
            with sp.Fori(2, B - 1) as b:
                iteration(b, 2, True)
            iteration(B - 1, 2, False)
            for b in (B - 2, B - 1):
                for t in range(NT):
                    store_out(b, t)
                    if b == B - 2:
                        load_residual(B - 1, t)
            for t in range(NT):
                sp.wait_ge(out_stored[t], 16 * B)

        @block.tensor
        def _(pe):
            def transposes(dst, src_of, n):
                for m in range(n):
                    last = nc.tensor.transpose(dst[:, m * P:(m + 1) * P], src_of(m), ident[:])
                return last

            def split_matmul(dst, left, right, chunks, beside=None):
                last = None
                for k in range(chunks):
                    if beside and k:
                        beside(k - 1)
                    for n, (a, m) in enumerate(term_pairs()):
                        last = nc.tensor.matmul(dst, left(a, k), right(m, k), start=(k == 0 and n == 0),
                                                stop=(k == chunks - 1 and n == 2))
                return last

            def transpose_xn(b, k, first=False):
                if not (first and k < 2):
                    pe.wait_ge(xnT_lo_ready, KC * b + k - 1)
                transposes(bank[6 + k % 2], lambda t: xn[:, t, k * P:(k + 1) * P], NT).then_inc(xt_done, 1)

            pe.wait_ge(ident_loaded, 16)
            pe.wait_ge(xn_ready, NT)
            for k in range(KC):
                transpose_xn(0, k, first=True)

            fq = raw[:, 1, :].rearrange("p (k e) -> p k e", k=KC)
            fo = raw[:, 2, :].rearrange("p (k e) -> p k e", k=KC)
            lv = raw[:, 3, 0:1024].rearrange("p (k e) -> p k e", k=KC)
            ro = raw[:, 3, 1024:2048].rearrange("p (k e) -> p k e", k=KC)

            def score_a(b, c, i, t):
                n = GB * 16 * b + 16 * c + 4 * i + t
                if isinstance(n, int) and n == 0:
                    stacks_free(pe)
                if i == 0 and t == 0:
                    pe.wait_ge(qk_loaded[c], 96 * b + 96)
                pe.wait_ge(max_taken, n + 1)
                nc.tensor.matmul(bank_a[t % 2][:], q_stack[0:STACK, c, i, t * P:(t + 1) * P],
                                 k_stack[0:STACK, c, i, :], start=True, stop=True).then_inc(pass_a_done, 1)

            def fold_weights(n, unit=None):
                dst = bank[6 + n % 2]
                if n == 0:
                    pe.wait_ge(ffn_w_loaded, 16 * 5)
                    pe.wait_ge(xnT_lo_ready, KC * B)
                if n >= 2:
                    pe.wait_ge(prep_taken, n - 1)
                for k in range(KC):
                    if n < KC:
                        last = nc.tensor.matmul(dst[:, 0:LEAVES], fq[:, k, n * P:(n + 1) * P], ro[:, k, :],
                                                start=k == 0, stop=k == KC - 1)
                    else:
                        h = n - KC
                        last = nc.tensor.matmul(dst[:], lv[:, k, h * P:(h + 1) * P], fo[:, k, :],
                                                start=k == 0, stop=k == KC - 1)
                    if k == KC - 1:
                        last.then_inc(prep_done, 1)
                    if unit is not None:
                        score_a(0, unit // HG, unit % HG, k)

            def batch(b, has_next, first=False):
                if first:
                    pe.wait_ge(w_lo["q"], 1)
                for c in range(KC):
                    pe.wait_ge(proj_taken, NPROJ * b + c + 1)
                    if c == 0:
                        pe.wait_ge(xnT_lo_ready, KC * b + KC)
                    split_matmul(bank[c][:], lambda a, k: w_in["q"][a][:, k, c * P:(c + 1) * P],
                                 lambda m, k: xnT[m][:, k, :], KC).then_inc(proj_done, 1)
                if first:
                    pe.wait_ge(w_lo["k"], 1)
                for c in range(KC):
                    pe.wait_ge(proj_taken, NPROJ * b + KC + c + 1)
                    if c == 0:
                        pe.wait_ge(cT_lo_ready, KC * b + KC)
                    split_matmul(bank[(KC + c) % 6][:], lambda a, k: w_in["k"][a][:, k, c * P:(c + 1) * P],
                                 lambda m, k: cT[m][:, k, :], KC).then_inc(proj_done, 1)
                    if has_next and c:
                        if c == 1:
                            pe.wait_ge(xn_ready, NT * b + 2 * NT)
                        transpose_xn(b + 1, c - 1)
                if first:
                    pe.wait_ge(w_lo["v"], 1)
                for t in range(NT):
                    pe.wait_ge(proj_taken, NPROJ * b + 2 * KC + t + 1)
                    split_matmul(bank[(2 * KC + t) % 6][:], lambda a, k: cT[a][:, k, t * P:(t + 1) * P],
                                 lambda m, k: w_in["v"][m][:, k, :], KC,
                                 beside=(lambda k: score_a(0, 0, t - 2, k)) if not has_next and t >= 2 else None
                                 ).then_inc(proj_done, 1)
                    if has_next and t == 1:
                        transpose_xn(b + 1, KC - 1)
                    if not has_next and t >= 2:
                        score_a(0, 0, t - 2, NT - 1)

            batch(0, True, first=True)
            with pe.Fori(1, B - 1) as b:
                batch(b, True)
            batch(B - 1, False)

            def score_b(b, c, j, i):
                n = GB * 16 * b + 16 * c + 4 * j + i
                if i == 0 and j == 0:
                    pe.wait_ge(maxrow_loaded, 16 * (GB * b + c + 1))
                pe.wait_ge(exp_done, n + 1)
                nc.tensor.matmul(bank_b[i % 2][:], k_stack[0:STACK + 1, c, i, j * P:(j + 1) * P],
                                 q_stack[0:STACK + 1, c, i, :], start=True, stop=True).then_inc(pass_b_done, 1)

            def prob_v(b, c, j):
                g = GB * b + c
                if j == 0:
                    pe.wait_ge(attn_taken, g + 1)
                    pe.wait_ge(v_loaded[c], 16 * b + 16)
                pe.wait_ge(exp_done, RING + 16 * g + 4 * j + 4)
                for i in range(HG):
                    last = nc.tensor.matmul(bank_pv[c % 2][DH * i:DH * (i + 1), :],
                                            v_sb[:, c, j, DH * i:DH * (i + 1)],
                                            prob[:, j, i * S:(i + 1) * S], start=j == 0, stop=j == NT - 1)
                last.then_inc(pv_done, 1)

            turns = Turns()
            readers = [[], []]

            def take_bank(kind, tile, *reader):
                s = turns.next
                for sema, value in readers[s]:
                    pe.wait_ge(sema, value)
                readers[s] = [reader]
                return turns.take(kind, tile)

            def transpose_max(b, c):
                g = GB * b + c
                dst = take_bank("max", c, negmax_ready, g + 1)
                pe.wait_ge(max_taken, RING + 16 * g + 16)
                nc.tensor.transpose(dst[0:HG * NT, 0:P], rowmax[:, c % 2, :], ident[:]).then_inc(max_transposed, 1)

            def denominators(b, c):
                g = GB * b + c
                dst = take_bank("den", c, lnden_done, g + 1)
                pe.wait_ge(pair_ready, 2 + 2 * g + 2)
                for h in range(2):
                    for i in range(HG):
                        last = nc.tensor.matmul(dst[DH * i:DH * (i + 1), :], ones[:], pair_sum[:, h, i * S:(i + 1) * S],
                                                start=h == 0, stop=h == 1)
                last.then_inc(den_done, 1)

            def project_out(b, t):
                dst = take_bank("o", t, x1_ready, NT * b + t + 1)
                pe.wait_ge(aT_lo_ready, GB * b + GB)
                split_matmul(dst[:], lambda a, k: aT[a][:, k, t * P:(t + 1) * P],
                             lambda m, k: wo[m][:, k, :], KC).then_inc(o_done, 1)

            def transpose_rn(b, t):
                dst = take_bank("rt", t, rnT_lo_ready, NT * b + t + 1)
                pe.wait_ge(rn_ready, NT * b + t + 1)
                transposes(dst, lambda k: rn[:, k * P:(k + 1) * P], KC).then_inc(rt_done, 1)

            def route(b, t):
                dst = take_bank("z", t, z_taken, NT * b + t + 1)
                pe.wait_ge(rnT_lo_ready, NT * b + t + 1)
                split_matmul(dst[:, 0:LEAVES], lambda a, k: rnT[a][:, k, :],
                             lambda m, k: wz[m][:, k, :], KC).then_inc(z_done, 1)

            def transpose_lp(b, t):
                dst = take_bank("lt", t, lpT_lo_ready, NT * b + t + 1)
                pe.wait_ge(tree_step, TREE_STEPS * b + DEPTH * (t // 2 + 1))
                transposes(dst, lambda h: lp[:, t, h * P:(h + 1) * P], LC).then_inc(lt_done, 1)

            def leaf_out(b, t):
                dst = take_bank("y", t, out_ready, NT * b + t + 1)
                pe.wait_ge(lpT_lo_ready, NT * b + t + 1)
                split_matmul(dst[:], lambda a, k: lpT[a][:, k, :], lambda m, k: wy[m][:, k, :], LC).then_inc(y_done, 1)

            side_jobs = {"o": project_out, "rt": transpose_rn, "z": route, "lt": transpose_lp, "y": leaf_out}

            def group_of(b, u):
                return b + u // TICKS, u % TICKS // NT

            def tick(b, u, back, has_next):
                c, j = u // NT, u % NT
                ahead = pass_a_unit(b, c, j, has_next)
                for half in range(2):
                    for i in (2 * half, 2 * half + 1):
                        score_b(b, c, j, i)
                        if ahead:
                            score_a(*ahead, i)
                    if half == 0 and (u or back):
                        prob_v(*group_of(b, u - 1), (j - 1) % NT)
                for kind, ago, n in side_at(u, back, has_next):
                    if kind == "max":
                        transpose_max(*group_of(b, NT * (n + 1)))
                    elif kind == "den":
                        denominators(*group_of(b, NT * (n - 1)))
                    else:
                        side_jobs[kind](b - ago, n)

            def iteration(b, back, has_next):
                known = [(negmax_ready, GB * b + 1)]
                if back:
                    known.append((lnden_done, GB * b - 1))
                    if back > 1:
                        known.append((z_taken, NT * (b - 1)))
                turns.next = 0
                readers[0], readers[1] = list(known), list(known)
                for u in range(TICKS):
                    tick(b, u, back, has_next)

            for n in range(N_PREP):
                fold_weights(n, 2 + n if 2 + n < A_LEAD else None)
                if n == 2:
                    pe.wait_ge(max_taken, RING + 16)
                    pe.wait_ge(proj_taken, PROJ_FREE + NPROJ * (B - 1) + 2 * KC + 1)
                    nc.tensor.transpose(bank[2][0:HG * NT, 0:P], rowmax[:, 0, :], ident[:]).then_inc(max_transposed, 1)
            pe.wait_ge(ones_row_set, GB)
            pe.wait_ge(prep_taken, N_PREP)
            phase0_over(pe)
            iteration(0, 0, True)
            iteration(1, 1, True)
            with pe.Fori(2, B - 1) as b:
                iteration(b, 2, True)
            iteration(B - 1, 2, False)

            last = B - 1
            prob_v(last, GB - 1, NT - 1)
            for t in range(NT):
                transpose_lp(last - 1, t)
                if t == 2:
                    denominators(last, GB - 1)
                leaf_out(last - 1, t)
            for t in range(NT):
                if t == 0:
                    pe.wait_ge(aT_lo_ready, GB * B)
                split_matmul(bank[t][:], lambda a, k: aT[a][:, k, t * P:(t + 1) * P],
                             lambda m, k: wo[m][:, k, :], KC).then_inc(o_done, 1)
            for t in range(NT):
                if t == 0:
                    pe.wait_ge(out_ready, NT * last)
                pe.wait_ge(rn_ready, NT * last + t + 1)
                transposes(bank[4 + t], lambda k: end_rn[:, t, k * P:(k + 1) * P], KC).then_inc(rt_done, 1)
            for t in range(NT):
                pe.wait_ge(rnT_lo_ready, NT * last + t + 1)
                split_matmul(bank[t][:, 0:LEAVES], lambda a, k: end_rnT[a][:, t, k * P:(k + 1) * P],
                             lambda m, k: wz[m][:, k, :], KC).then_inc(z_done, 1)
            pe.wait_ge(tree_step, TREE_STEPS * B)
            for t in range(NT):
                transposes(bank[4 + t], lambda h: lp[:, t, h * P:(h + 1) * P], LC).then_inc(lt_done, 1)
            for t in range(NT):
                pe.wait_ge(lpT_lo_ready, NT * last + t + 1)
                split_matmul(bank[t][:], lambda a, k: end_lpT[a][:, t, k * P:(k + 1) * P],
                             lambda m, k: wy[m][:, k, :], LC).then_inc(y_done, 1)

        @block.scalar
        def _(act):
            act.wait_ge(gates_loaded, 32)
            nc.scalar.activation(gain[:], gates_in[:], ACT.Tanh).then_inc(tanh_done, 1)
            nc.scalar.preload_act_table_set("natural_log_exp_and_others")
            act.wait_ge(consts_set, 2)

            def rstd(b):
                act.wait_ge(mv_done, NT * b + NT)
                nc.scalar.activation(x_lnv[:], x_mv[:, :, 1], ACT.Ln, bias=eps[:]).then_inc(lnv_done, 1)
                act.wait_ge(lnv_done, b + 1)
                nc.scalar.activation(x_rstd[:], x_lnv[:], ACT.Exp, scale=-0.5).then_inc(rstd_done, 1)

            def evac_xt(b, k):
                act.wait_ge(xt_done, KC * b + k + 1)
                nc.scalar.copy(xnT[0][:, k, :], bank[6 + k % 2][:]).then_inc(xnT_hi_ready, 1)

            def evac_proj(b, n, c, first):
                act.wait_ge(proj_done, NPROJ * b + first + c + 1)
                act.wait_ge(stored[n][c % 2], STAGE_FREE + 32 * (2 * b + c // 2))
                nc.scalar.activation(stage[n][0][:, c % 2, :], bank[(first + c) % 6][:], ACT.Identity,
                                     bias=(b_q if n == "q" else b_k)[:, c:c + 1]).then_inc(proj_hi_staged, 1)

            def weight_hi(n, slot, dst):
                nc.scalar.copy(dst[0][:].rearrange("p k e -> p (k e)"), raw[:, slot, :]).then_inc(w_hi[n], 1)

            rstd(0)
            act.wait_ge(w_loaded[0], 16)
            weight_hi("q", 0, w_in["q"])
            for k in range(KC):
                evac_xt(0, k)

            def hi_folded(n):
                act.wait_ge(prep_done, n + 1)
                if n < KC:
                    nc.scalar.copy(wz[0][:, n, :], bank[6 + n % 2][:, 0:LEAVES]).then_inc(prep_hi, 1)
                else:
                    nc.scalar.copy(wy[0][:, n - KC, :], bank[6 + n % 2][:]).then_inc(prep_hi, 1)

            def batch(b, has_next, first=False):
                act.wait_ge(c_loaded, 16 * b + 16)
                if not isinstance(b, int) or b:
                    act.wait_ge(proj_done, NPROJ * b)
                for k in range(KC):
                    nc.scalar.copy(cT[0][:, k, :], c_in[:, k, :]).then_inc(cT_hi_ready, 1)
                if first:
                    for slot, n in ((1, "k"), (2, "v")):
                        act.wait_ge(w_loaded[slot], 16)
                        weight_hi(n, slot, w_in[n])
                    act.wait_ge(small_loaded, 16 * 5)
                if has_next and not first:
                    rstd(b + 1)
                if not has_next:
                    act.wait_ge(ffn_w_loaded, 16 * 5)
                    weight_hi("o", 0, wo)
                for c in range(KC):
                    evac_proj(b, "q", c, 0)
                    if first and c == 2:
                        rstd(b + 1)
                for c in range(KC):
                    evac_proj(b, "k", c, KC)
                    if has_next and c:
                        evac_xt(b + 1, c - 1)
                if has_next:
                    evac_xt(b + 1, KC - 1)

            batch(0, True, first=True)
            with act.Fori(1, B - 1) as b:
                batch(b, True)
            batch(B - 1, False)

            def row_of_maxima(b, c, src, first=False):
                g = GB * b + c
                act.wait_ge(max_transposed, g + 1)
                if not first:
                    act.wait_ge(maxrow_loaded, 16 * g)
                nc.scalar.mul(negmax[:], src[0:HG * NT, 0:P], -1.0).then_inc(negmax_ready, 1)
                act.wait_ge(negmax_ready, g + 1)
                act.dma_start(q_stack[STACK:STACK + 1, c, :, :].rearrange("o i (t q) -> o (i t) q", q=P).bitcast(F32),
                              negmax[:].bitcast(F32)).then_inc(maxrow_loaded, 16)

            for n in range(N_PREP):
                hi_folded(n)
                if n == 2:
                    row_of_maxima(0, 0, bank[2], first=True)

            turns = Turns()

            def exp_scores(b, c, j, i):
                g = GB * b + c
                n = 16 * g + 4 * j + i
                act.wait_ge(pass_b_done, n + 1)
                if i == 0:
                    act.wait_ge(pv_done, 4 * g + j + 1)
                    act.wait_ge(pair_ready, 2 * g + j // 2 + 1)
                nc.scalar.activation(prob[:, j, i * S:(i + 1) * S], bank_b[i % 2][:], ACT.Exp,
                                     scale=SCALE).then_inc(exp_done, 1)

            def invert_denominators(b, c, src):
                g = GB * b + c
                act.wait_ge(den_done, 1 + g + 1)
                act.wait_ge(attn_taken, RING + g)
                nc.scalar.activation(inv_den[:], src[:], ACT.Ln).then_inc(lnden_done, 1)
                act.wait_ge(lnden_done, g + 1)
                nc.scalar.activation(inv_den[:], inv_den[:], ACT.Exp, scale=-1.0).then_inc(invden_ready, 1)

            def hi_attn(b, c):
                act.wait_ge(attn_taken, RING + GB * b + c + 1)
                if not isinstance(b, int) or b:
                    act.wait_ge(o_done, NT * b)
                nc.scalar.copy(aT[0][:, c, :], attn[:]).then_inc(aT_hi_ready, 1)

            def rstd1(b):
                act.wait_ge(r_mv_done, NT * b + NT)
                nc.scalar.activation(r_lnv[:], r_mv[:, :, 1], ACT.Ln, bias=eps[:]).then_inc(r_lnv_done, 1)
                act.wait_ge(r_lnv_done, b + 1)
                nc.scalar.activation(r_rstd[:], r_lnv[:], ACT.Exp, scale=-0.5).then_inc(r_rstd_done, 1)

            def normalise1(b, t, dst):
                n = NT * b + t
                act.wait_ge(r_shift_done, b + 1)
                if dst is rn and (not isinstance(b, int) or n):
                    act.wait_ge(rt_done, n)
                nc.scalar.activation(dst[:], res[:, t, :], ACT.Identity, bias=r_shift[:, t:t + 1],
                                     scale=r_rstd[:, t:t + 1]).then_inc(rn_ready, 1)

            def evac_rt(b, t, src, dst, shared=True):
                n = NT * b + t
                act.wait_ge(rt_done, n + 1)
                if shared:
                    act.wait_ge(z_done, 1 + n)
                nc.scalar.copy(dst, src[:]).then_inc(rnT_hi_ready, 1)

            def sigmoid(b, h, step):
                n = PAIRS * b + h
                tiles = gate[:, 2 * h:2 * h + 2, :]
                if step == 0:
                    act.wait_ge(z_taken, 2 * n + 2)
                else:
                    act.wait_ge(sig_step, 3 * n + step)
                if step == 0:
                    nc.scalar.activation(tiles, tiles, ACT.Exp, scale=-1.0).then_inc(sig_step, 1)
                elif step == 1:
                    nc.scalar.activation(tiles, tiles, ACT.Ln, bias=one_col).then_inc(sig_step, 1)
                elif step == 2:
                    nc.scalar.activation(tiles, tiles, ACT.Exp, scale=-1.0).then_inc(sig_step, 1)
                else:
                    nc.scalar.activation(ungate[:, 2 * h:2 * h + 2, :], tiles, ACT.Identity, bias=one_col,
                                         scale=-1.0).then_inc(gates_ready, 1)

            def evac_lt(b, t, src, dst):
                n = NT * b + t
                act.wait_ge(lt_done, n + 1)
                if dst is lpT[0]:
                    act.wait_ge(y_done, 1 + n)
                    dst = dst[:].rearrange("p k q -> p (k q)")
                nc.scalar.copy(dst, src[:, 0:LC * P]).then_inc(lpT_hi_ready, 1)

            one_col = ones[:, 0:1]

            def group_of(b, u):
                return b + u // TICKS, u % TICKS // NT

            def side_work(b, entries):
                for kind, ago, t in entries:
                    if kind == "rt":
                        evac_rt(b - ago, t, turns.where["rt", t], rnT[0][:].rearrange("p k q -> p (k q)"))
                    if kind == "lt":
                        evac_lt(b - ago, t, turns.where["lt", t], lpT[0])

            def tick(b, u, back, has_next, waiting):
                c, j = u // NT, u % NT
                side_work(*waiting)
                for i in range(HG):
                    exp_scores(b, c, j, i)
                    if i == 1 and j == 0 and (c >= 2 or back):
                        hi_attn(*group_of(b, u - NT - 1))
                    if i == 1 and back and u == RSTD_TICK:
                        rstd1(b - 1)
                    if i == 2 and back and RN_TICK <= u < RN_TICK + NT:
                        normalise1(b - 1, u - RN_TICK, rn)
                    if (u, i) in SIGMOID_AT:
                        ago, h, step = SIGMOID_AT[u, i]
                        if ago <= back:
                            sigmoid(b - ago, h, step)
                entries = side_at(u, back, has_next)
                for kind, ago, n in entries:
                    src = turns.take(kind, n)
                    if kind == "max":
                        row_of_maxima(*group_of(b, NT * (n + 1)), src)
                    if kind == "den":
                        invert_denominators(*group_of(b, NT * (n - 1)), src)
                return b, entries

            def iteration(b, back, has_next):
                turns.next = 0
                waiting = (b, [])
                for u in range(TICKS):
                    waiting = tick(b, u, back, has_next, waiting)
                side_work(*waiting)

            phase0_over(act)
            act.wait_ge(w_lo["o"], 1)
            iteration(0, 0, True)
            iteration(1, 1, True)
            with act.Fori(2, B - 1) as b:
                iteration(b, 2, True)
            iteration(B - 1, 2, False)

            last = B - 1
            for t in range(NT):
                if t == 0:
                    sigmoid(last - 1, 1, 2)
                    sigmoid(last - 1, 1, 3)
                    hi_attn(last, GB - 2)
                evac_lt(last - 1, t, turns.take("lt", t), lpT[0])
                if t == 2:
                    invert_denominators(last, GB - 1, turns.take("den", GB - 1))
                turns.take("y", t)
            hi_attn(last, GB - 1)
            rstd1(last)
            for t in range(NT):
                normalise1(last, t, end_rn[:, t, :])
            for t in range(NT):
                evac_rt(last, t, bank[4 + t], end_rnT[0][:, t, :], shared=False)
            for h in range(PAIRS):
                for step in range(4):
                    sigmoid(last, h, step)
            for t in range(NT):
                evac_lt(last, t, bank[4 + t], end_lpT[0][:, t, 0:LC * P])

        @block.vector
        def _(dve):
            nc.vector.memset(ones[:], 1.0).then_inc(consts_set, 1)
            nc.vector.memset(eps[:], LN_EPS).then_inc(consts_set, 1)
            dve.sem_inc(proj_taken, PROJ_FREE)
            dve.sem_inc(max_taken, RING)
            dve.sem_inc(attn_taken, RING)

            def statistics(b):
                dve.wait_ge(x_loaded, 16 * b + 16)
                for t in range(NT):
                    nc.vector.bn_stats(x_stats[:, t, :], x_in[:, t, :]).then_inc(stats_done, 1)
                dve.wait_ge(stats_done, NT * b + NT)
                dve.sem_inc(stats_seen, 1)
                for t in range(NT):
                    nc.vector.bn_aggr(x_mv[:, t, :], x_stats[:, t, :]).then_inc(mv_done, 1)

            def normalise(b, first=False):
                dve.wait_ge(rstd_done, b + 1)
                if not first:
                    dve.wait_ge(xt_done, KC * b)
                for t in range(NT):
                    nc.vector.tensor_scalar(xn[:, t, :], x_in[:, t, :], x_mv[:, t, 0:1], x_rstd[:, t:t + 1],
                                            ALU.subtract, ALU.mult).then_inc(xn_ready, 1)

            def lo_xt(b, k):
                dve.wait_ge(xnT_hi_ready, KC * b + k + 1)
                nc.vector.tensor_tensor(xnT[1][:, k, :], bank[6 + k % 2][:], xnT[0][:, k, :].bitcast(F32),
                                        ALU.subtract).then_inc(xnT_lo_ready, 1)

            statistics(0)
            normalise(0, first=True)
            dve.wait_ge(w_hi["q"], 1)
            nc.vector.tensor_tensor(w_in["q"][1][:].rearrange("p k e -> p (k e)"), raw[:, 0, :],
                                    w_in["q"][0][:].rearrange("p k e -> p (k e)").bitcast(F32),
                                    ALU.subtract).then_inc(w_lo["q"], 1)
            for k in range(KC):
                lo_xt(0, k)

            def lo_proj(b, n, c, first):
                done = (NPROJ - NT) * b + first + c + 1
                dve.wait_ge(proj_hi_staged, done)
                nc.vector.scalar_tensor_tensor(
                    out=stage[n][1][:, c % 2, :], in0=bank[(first + c) % 6][:],
                    scalar=(b_q if n == "q" else b_k)[:, c:c + 1], in1=stage[n][0][:, c % 2, :].bitcast(F32),
                    op0=ALU.add, op1=ALU.subtract).then_inc(proj_taken, 1)

            def lo_folded(n):
                dve.wait_ge(prep_hi, n + 1)
                if n < KC:
                    hi, lo, src = wz[0][:, n, :], wz[1][:, n, :], bank[6 + n % 2][:, 0:LEAVES]
                else:
                    hi, lo, src = wy[0][:, n - KC, :], wy[1][:, n - KC, :], bank[6 + n % 2][:]
                nc.vector.tensor_tensor(lo, src, hi.bitcast(F32), ALU.subtract).then_inc(prep_taken, 1)

            def row_max(b, c, i, t):
                n = GB * 16 * b + 16 * c + 4 * i + t
                dve.wait_ge(pass_a_done, n + 1)
                nc.vector.reduce_max(rowmax[:, c % 2, 4 * i + t:4 * i + t + 1], bank_a[t % 2][:], AX_X
                                     ).then_inc(max_taken, 1)

            def batch(b, has_next, first=False):
                if not has_next:
                    dve.wait_ge(w_hi["o"], 1)
                    nc.vector.tensor_tensor(wo[1][:].rearrange("p k e -> p (k e)"), raw[:, 0, :],
                                            wo[0][:].rearrange("p k e -> p (k e)").bitcast(F32),
                                            ALU.subtract).then_inc(w_lo["o"], 1)
                if has_next and not first:
                    statistics(b + 1)
                for c in range(KC):
                    lo_proj(b, "q", c, 0)
                    if first and c == 1:
                        statistics(b + 1)
                    if has_next and c == (3 if first else 1):
                        normalise(b + 1)
                for c in range(KC):
                    lo_proj(b, "k", c, KC)
                    if has_next and c:
                        lo_xt(b + 1, c - 1)
                if first:
                    dve.wait_ge(w_lo["k"], 1)
                    dve.wait_ge(w_lo["v"], 1)
                    nc.vector.memset(raw[:, 3, 1024:2048], 0.0).then_inc(raw_cleared, 1)
                    dve.wait_ge(tanh_done, 1)
                    nc.vector.tensor_scalar(g_bo[:], g_bo[:], gain[:, 0:1], None, ALU.mult).then_inc(consts_set, 1)
                    nc.vector.tensor_scalar(g_wb[:], g_wb[:], gain[:, 1:2], None, ALU.mult).then_inc(consts_set, 1)
                for t in range(NT):
                    if has_next and t == 2:
                        lo_xt(b + 1, KC - 1)
                    if not has_next and t >= 2:
                        for q in range(NT):
                            row_max(0, 0, t - 2, q)
                    dve.wait_ge(proj_done, NPROJ * b + 2 * KC + t + 1)
                    dve.wait_ge(stored["v"][t % 2], STAGE_FREE + 16 * (2 * b + t // 2))
                    nc.vector.tensor_tensor(stage_v[:, t % 2, :], bank[(2 * KC + t) % 6][:], b_v[:],
                                            ALU.add).then_inc(proj_taken, 1)

            dve.wait_ge(small_loaded, 16 * 5)
            batch(0, True, first=True)
            with dve.Fori(1, B - 1) as b:
                batch(b, True)
            batch(B - 1, False)

            turns = Turns()

            def normalise_attn(b, c):
                g = GB * b + c
                dve.wait_ge(invden_ready, g + 1)
                dve.wait_ge(aT_lo_ready, g) if not isinstance(b, int) or g else None
                nc.vector.tensor_tensor(attn[:], bank_pv[c % 2][:], inv_den[:], ALU.mult).then_inc(attn_taken, 1)

            def add_attn(b, t, src):
                n = NT * b + t
                dve.wait_ge(o_done, n + 1)
                dve.wait_ge(res_biased, n + 1)
                nc.vector.scalar_tensor_tensor(out=res[:, t, :], in0=src[:], scalar=gain[:, 0:1],
                                               in1=res[:, t, :], op0=ALU.mult, op1=ALU.add).then_inc(x1_ready, 1)

            def x1_statistics(b, t):
                n = NT * b + t
                dve.wait_ge(x1_ready, n + 1)
                nc.vector.bn_stats(r_stats[:, t, :], res[:, t, :]).then_inc(r_stats_done, 1)
                dve.wait_ge(r_stats_done, n + 1)
                dve.sem_inc(stats_seen, 1)
                nc.vector.bn_aggr(r_mv[:, t, :], r_stats[:, t, :]).then_inc(r_mv_done, 1)

            def shift(b):
                dve.wait_ge(r_rstd_done, b + 1)
                nc.vector.scalar_tensor_tensor(out=r_shift[:], in0=r_mv[:, :, 0], scalar=-1.0, in1=r_rstd[:],
                                               op0=ALU.mult, op1=ALU.mult).then_inc(r_shift_done, 1)

            def lo_rt(b, t, src, hi, lo):
                dve.wait_ge(rnT_hi_ready, NT * b + t + 1)
                nc.vector.tensor_tensor(lo, src[:], hi.bitcast(F32), ALU.subtract).then_inc(rnT_lo_ready, 1)

            def take_z(b, t, src):
                n = NT * b + t
                dve.wait_ge(z_done, 1 + n + 1)
                if not isinstance(b, int) or b:
                    dve.wait_ge(tree_step, TREE_STEPS * b)
                nc.vector.tensor_scalar(gate[:, t, :], src[:, 0:LEAVES], Z_FLOOR, None, ALU.max
                                        ).then_inc(z_taken, 1)

            def tree_levels(b, h, levels):
                tiles = slice(2 * h, 2 * h + 2)
                if 0 in levels:
                    dve.wait_ge(gates_ready, PAIRS * b + h + 1)
                    if h == 0 and (not isinstance(b, int) or b):
                        dve.wait_ge(lt_done, NT * b)
                for level in levels:
                    n = 1 << level
                    parents, children = (lp_odd, lp) if (DEPTH - 1 - level) % 2 == 0 else (lp, lp_odd)
                    dst = children[:, tiles, 0:2 * n].rearrange("p t (m two) -> p t m two", two=2)
                    g1 = gate[:, tiles, n - 1:2 * n - 1]
                    g0 = ungate[:, tiles, n - 1:2 * n - 1]
                    if level == 0:
                        nc.vector.tensor_copy(dst[:, :, :, 0], g0)
                        last = nc.vector.tensor_copy(dst[:, :, :, 1], g1)
                    else:
                        dve.wait_ge(tree_step, TREE_STEPS * b + DEPTH * h + level)
                        nc.vector.tensor_tensor(dst[:, :, :, 0], parents[:, tiles, 0:n], g0, ALU.mult)
                        last = nc.vector.tensor_tensor(dst[:, :, :, 1], parents[:, tiles, 0:n], g1, ALU.mult)
                    last.then_inc(tree_step, 1)

            def lo_lt(b, t, src, hi, lo):
                dve.wait_ge(lpT_hi_ready, NT * b + t + 1)
                nc.vector.tensor_tensor(lo, src[:, 0:LC * P], hi.bitcast(F32), ALU.subtract
                                        ).then_inc(lpT_lo_ready, 1)

            def add_ffn(b, t, src):
                n = NT * b + t
                dve.wait_ge(y_done, 1 + n + 1)
                dve.wait_ge(x1_biased, n + 1)
                nc.vector.scalar_tensor_tensor(out=res[:, t, :], in0=src[:], scalar=gain[:, 1:2],
                                               in1=res[:, t, :], op0=ALU.mult, op1=ALU.add).then_inc(out_ready, 1)

            def group_of(b, u):
                return b + u // TICKS, u % TICKS // NT

            def flat(parts, s):
                return parts[s][:].rearrange("p k q -> p (k q)")

            def side_work(b, entries):
                for kind, ago, t in entries:
                    src = turns.where[kind, t]
                    if kind == "o":
                        add_attn(b - ago, t, src)
                    if kind == "rt":
                        lo_rt(b - ago, t, src, flat(rnT, 0), flat(rnT, 1))
                    if kind == "z":
                        take_z(b - ago, t, src)
                    if kind == "lt":
                        lo_lt(b - ago, t, src, flat(lpT, 0), flat(lpT, 1))
                    if kind == "y":
                        add_ffn(b - ago, t, src)

            def tick(b, u, back, has_next, waiting):
                c, j = u // NT, u % NT
                ahead = pass_a_unit(b, c, j, has_next)
                for t in range(NT):
                    if ahead:
                        row_max(*ahead, t)
                    if t == 1:
                        side_work(*waiting)
                    if t == 3 and j == NT - 1 and (c or back):
                        normalise_attn(*group_of(b, u - NT))
                    if t == 3 and back and u == RSTD_TICK:
                        shift(b - 1)
                    if t == 3:
                        for kind, ago, m in waiting[1]:
                            if kind == "o":
                                x1_statistics(b - ago, m)
                    if (u, t) in TREE_AT:
                        ago, h, levels = TREE_AT[u, t]
                        if ago <= back:
                            tree_levels(b - ago, h, levels)
                entries = side_at(u, back, has_next)
                for kind, ago, n in entries:
                    turns.take(kind, n)
                return b, entries

            def iteration(b, back, has_next):
                turns.next = 0
                waiting = (b, [])
                for u in range(TICKS):
                    waiting = tick(b, u, back, has_next, waiting)
                side_work(*waiting)

            for n in range(N_PREP):
                if 2 + n < A_LEAD:
                    for t in range(NT):
                        row_max(0, (2 + n) // HG, (2 + n) % HG, t)
                lo_folded(n)
            phase0_over(dve)
            iteration(0, 0, True)
            iteration(1, 1, True)
            with dve.Fori(2, B - 1) as b:
                iteration(b, 2, True)
            iteration(B - 1, 2, False)

            last = B - 1
            tree_levels(last - 1, 1, range(DEPTH))
            for t in range(NT):
                lo_lt(last - 1, t, turns.take("lt", t), flat(lpT, 0), flat(lpT, 1))
                if t == 2:
                    turns.take("den", GB - 1)
                add_ffn(last - 1, t, turns.take("y", t))
            normalise_attn(last, GB - 1)
            for t in range(NT):
                add_attn(last, t, bank[t])
                x1_statistics(last, t)
            shift(last)
            for t in range(NT):
                lo_rt(last, t, bank[4 + t], end_rnT[0][:, t, :], end_rnT[1][:, t, :])
            for t in range(NT):
                take_z(last, t, bank[t])
            for h in range(PAIRS):
                tree_levels(last, h, range(DEPTH))
            for t in range(NT):
                lo_lt(last, t, bank[4 + t], end_lpT[0][:, t, 0:LC * P], end_lpT[1][:, t, 0:LC * P])
            for t in range(NT):
                add_ffn(last, t, bank[t])

        @block.gpsimd
        def _(pool):
            def batch(b):
                for k in range(KC):
                    pool.wait_ge(cT_hi_ready, KC * b + k + 1)
                    nc.gpsimd.tensor_tensor(cT[1][:, k, :], c_in[:, k, :], cT[0][:, k, :].bitcast(F32),
                                            ALU.subtract).then_inc(cT_lo_ready, 1)

            def weight_lo(n, slot):
                pool.wait_ge(w_hi[n], 1)
                nc.gpsimd.tensor_tensor(w_in[n][1][:].rearrange("p k e -> p (k e)"), raw[:, slot, :],
                                        w_in[n][0][:].rearrange("p k e -> p (k e)").bitcast(F32),
                                        ALU.subtract).then_inc(w_lo[n], 1)

            batch(0)
            weight_lo("k", 1)
            weight_lo("v", 2)
            with pool.Fori(1, B) as b:
                batch(b)

            stacks_free(pool)
            for c in range(GB):
                nc.gpsimd.memset(k_stack[STACK:STACK + 1, c, :, :].bitcast(F32), 1.0).then_inc(ones_row_set, 1)
            phase0_over(pool)
            pool.sem_inc(exp_done, RING)
            pool.sem_inc(pv_done, NT)
            pool.sem_inc(pair_ready, 2)
            pool.sem_inc(den_done, 1)
            pool.sem_inc(z_done, 1)
            pool.sem_inc(y_done, 1)

            def add_pair(b, c, h):
                g = GB * b + c
                pool.wait_ge(exp_done, RING + 16 * g + 8 * h + 8)
                pool.wait_ge(den_done, g + 1)
                nc.gpsimd.tensor_tensor(pair_sum[:, h, :], prob[:, 2 * h, :], prob[:, 2 * h + 1, :],
                                        ALU.add).then_inc(pair_ready, 1)

            def lo_attn(b, c):
                pool.wait_ge(aT_hi_ready, GB * b + c + 1)
                nc.gpsimd.tensor_tensor(aT[1][:, c, :], attn[:], aT[0][:, c, :].bitcast(F32),
                                        ALU.subtract).then_inc(aT_lo_ready, 1)

            def bias_residual(b, t):
                pool.wait_ge(res_loaded[t], 16 * b + 16)
                nc.gpsimd.tensor_tensor(res[:, t, :], res[:, t, :], g_bo[:], ALU.add).then_inc(res_biased, 1)

            def bias_x1(b, t):
                pool.wait_ge(rn_ready, NT * b + t + 1)
                nc.gpsimd.tensor_tensor(res[:, t, :], res[:, t, :], g_wb[:], ALU.add).then_inc(x1_biased, 1)

            def iteration(b, back):
                for c in range(GB):
                    if back and c == 1:
                        bias_residual(b - 1, 0)
                    if back or c >= 2:
                        lo_attn(b if c >= 2 else b - 1, (c - 2) % GB)
                    if back or c:
                        add_pair(b if c else b - 1, (c - 1) % GB, 1)
                    if back and c == 1:
                        for t in range(1, NT):
                            bias_residual(b - 1, t)
                    add_pair(b, c, 0)
                if back:
                    for t in range(NT):
                        bias_x1(b - 1, t)

            pool.wait_ge(consts_set, 4)
            iteration(0, 0)
            with pool.Fori(1, B) as b:
                iteration(b, 1)
            lo_attn(B - 1, GB - 2)
            add_pair(B - 1, GB - 1, 1)
            lo_attn(B - 1, GB - 1)
            for t in range(NT):
                bias_residual(B - 1, t)
            for t in range(NT):
                bias_x1(B - 1, t)


def kernel(x, ctx_1024, g_xattn, g_ffn, L0_xattn_Wq, L0_xattn_bq, L0_xattn_Wk, L0_xattn_bk, L0_xattn_Wv,
           L0_xattn_bv, L0_xattn_Wo, L0_xattn_bo, L0_ffn_Wq, L0_ffn_routers, L0_ffn_leaf_keys,
           L0_ffn_leaf_values, L0_ffn_Wout_w, L0_ffn_Wout_b):
    import numpy as _np
    import concourse.bacc as _bacc
    from concourse import mybir as _mybir
    from concourse.bass_utils import run_bass_kernel_spmd as _run

    def laid(a):
        return _np.ascontiguousarray(a)

    def columns(v):
        return _np.asarray(v).reshape(-1, 128).T

    given = {
        "x": x,
        "ctxT": _np.asarray(ctx_1024).transpose(0, 2, 1),
        "g_xattn": g_xattn,
        "g_ffn": g_ffn,
        "WqT": _np.asarray(L0_xattn_Wq).T,
        "bq": columns(L0_xattn_bq),
        "WkT": _np.asarray(L0_xattn_Wk).T,
        "bk": columns(L0_xattn_bk),
        "WvT": _np.asarray(L0_xattn_Wv).T,
        "bv": L0_xattn_bv,
        "WoT": _np.asarray(L0_xattn_Wo).T,
        "bo": L0_xattn_bo,
        "ffn_Wq": L0_ffn_Wq,
        "routersT": _np.asarray(L0_ffn_routers).T,
        "leaf_valuesT": _np.asarray(L0_ffn_leaf_values).T,
        "WoutT": _np.asarray(L0_ffn_Wout_w).T,
        "Wout_b": L0_ffn_Wout_b,
        "ident": _np.eye(128, dtype=_np.float32),
    }
    nc = _bacc.Bacc("TRN2", target_bir_lowering=False, num_devices=1)
    arrays, args = {}, []
    for name, a in given.items():
        a = laid(a)
        arrays[f"in_{name}"] = a
        args.append(nc.dram_tensor(f"in_{name}", a.shape, _mybir.dt.from_np(a.dtype), kind="ExternalInput").ap())
    args.append(nc.dram_tensor("out_x", x.shape, _mybir.dt.float32, kind="ExternalOutput").ap())
    gated_block(nc, *args)
    r = _run(nc, [arrays], core_ids=[0])
    return r.results[0]["out_x"]
```

```python
from contextlib import ExitStack

import concourse.bass as bass
from concourse import mybir

F32 = mybir.dt.float32
F32R = mybir.dt.float32r
ALU = mybir.AluOpType
ACT = mybir.ActivationFunctionType
AX_X = mybir.AxisListType.X

P = 128
LN_EPS = 1e-5
Z_FLOOR = -40.0


def gated_block(nc, x, ctxT, g_xattn, g_ffn, WqT, bq, WkT, bk, WvT, bv, WoT, bo,
                ffn_Wq, routersT, leaf_valuesT, WoutT, Wout_b, ident_in, out):
    B, S, D = x.shape
    H = 16
    DH = D // H
    KC = D // P
    HG = P // DH
    NT = S // P
    GB = H // HG
    NODES = routersT.shape[1]
    LEAVES = NODES + 1
    LC = LEAVES // P
    DEPTH = LEAVES.bit_length() - 1
    SCALE = float(DH) ** -0.5
    STACK = 3 * DH
    assert KC == HG == NT == GB == 4 and DH == 32

    qT_dram = nc.dram_tensor("qT_split", (B, GB, 2, DH, HG, S), F32).ap()
    kT_dram = nc.dram_tensor("kT_split", (B, GB, 2, DH, HG, S), F32).ap()
    v_dram = nc.dram_tensor("v_by_group", (B, GB, P, NT, P), F32).ap()

    with ExitStack() as ctx:
        def sem(name):
            return ctx.enter_context(nc.semaphore(name))

        def sb(name, shape, dt, stack=ctx):
            return stack.enter_context(nc.sbuf_tensor(name, shape, dt))

        raw = sb("raw", [P, 4, 2048], F32)
        wo = [sb(f"wo_{s}", [P, KC, D], F32R) for s in ("hi", "lo")]
        wz = [sb(f"wz_{s}", [P, KC, LEAVES], F32R) for s in ("hi", "lo")]
        wy = [sb(f"wy_{s}", [P, LC, D], F32R) for s in ("hi", "lo")]
        ident = sb("ident", [P, P], F32)
        ones = sb("ones", [P, DH], F32)
        gates_in = sb("gates_in", [P, 2], F32)
        gain = sb("gain", [P, 2], F32)
        eps = sb("eps", [P, 1], F32)
        g_bo = sb("g_bo", [P, D], F32)
        g_wb = sb("g_wb", [P, D], F32)

        rowmax = sb("rowmax", [P, 2, HG * NT], F32)
        negmax = sb("negmax", [HG * NT, P], F32R)

        phase0 = ExitStack()
        w_in = {"q": [sb(f"wq_{s}", [P, KC, D], F32R, phase0) for s in ("hi", "lo")]}
        xnT = [sb(f"xnT_{s}", [P, KC, S], F32R, phase0) for s in ("hi", "lo")]
        x_in = sb("x_in", [P, NT, D], F32, phase0)
        xn = sb("xn", [P, NT, D], F32, phase0)
        w_in["k"] = [sb(f"wk_{s}", [P, KC, D], F32R, phase0) for s in ("hi", "lo")]
        c_in = sb("c_in", [P, KC, S], F32, phase0)
        w_in["v"] = [sb(f"wv_{s}", [P, KC, D], F32R, phase0) for s in ("hi", "lo")]
        b_q = sb("b_q", [P, KC], F32, phase0)
        b_k = sb("b_k", [P, KC], F32, phase0)
        b_v = sb("b_v", [P, D], F32, phase0)
        x_stats = sb("x_stats", [P, NT, 6], F32, phase0)
        x_mv = sb("x_mv", [P, NT, 2], F32, phase0)
        x_lnv = sb("x_lnv", [P, NT], F32, phase0)
        x_rstd = sb("x_rstd", [P, NT], F32, phase0)
        cT = [sb(f"cT_{s}", [P, KC, S], F32R, phase0) for s in ("hi", "lo")]
        stage = {n: [sb(f"stage_{n}_{s}", [P, 2, S], F32R, phase0) for s in ("hi", "lo")] for n in "qk"}
        stage_v = sb("stage_v", [P, 2, D], F32, phase0)
        phase0.close()

        q_stack = sb("q_stack", [P, GB, HG, S], F32R)
        k_stack = sb("k_stack", [P, GB, HG, S], F32R)
        v_sb = sb("v_sb", [P, GB, NT, P], F32)
        prob = raw
        pair_sum = sb("pair_sum", [P, 2, HG * S], F32)
        inv_den = sb("inv_den", [P, S], F32)
        attn = sb("attn", [P, S], F32)
        aT = [sb(f"aT_{s}", [P, GB, S], F32R) for s in ("hi", "lo")]
        res = sb("res", [P, NT, D], F32)
        r_stats = sb("r_stats", [P, NT, 6], F32)
        r_mv = sb("r_mv", [P, NT, 2], F32)
        r_lnv = sb("r_lnv", [P, NT], F32)
        r_rstd = sb("r_rstd", [P, NT], F32)
        r_shift = sb("r_shift", [P, NT], F32)
        rn = sb("rn", [P, D], F32)
        rnT = [sb(f"rnT_{s}", [P, KC, P], F32R) for s in ("hi", "lo")]
        gate = sb("gate", [P, NT, LEAVES], F32)
        ungate = sb("ungate", [P, NT, LEAVES], F32)
        lp_odd = sb("lp_odd", [P, NT, LEAVES // 2], F32)
        lp = sb("lp", [P, NT, LEAVES], F32)
        lpT = [sb(f"lpT_{s}", [P, LC, P], F32R) for s in ("hi", "lo")]

        end_rn = pair_sum[:, 0, :].rearrange("p (t d) -> p t d", t=NT)
        end_rnT = [q_stack[:, 0, :, :], q_stack[:, 1, :, :]]
        end_lpT = [q_stack[:, 2, :, :], q_stack[:, 3, :, :]]

        bank = [ctx.enter_context(nc.psum_tensor(f"bank{i}", [P, 512], F32)) for i in range(8)]
        bank_a, bank_b, bank_pv, bank_g = bank[0:2], bank[2:4], bank[4:6], bank[6:8]
        END_Y_BANK, END_DEN_BANK = (bank[4], bank[6], bank[2], bank[3]), bank[7]

        w_loaded = [sem(f"w_loaded_{n}") for n in "qkv"]
        small_loaded = sem("small_loaded")
        ffn_w_loaded = sem("ffn_w_loaded")
        consts_set = sem("consts_set")
        gates_loaded = sem("gates_loaded")
        ident_loaded = sem("ident_loaded")
        raw_cleared = sem("raw_cleared")
        tanh_done = sem("tanh_done")
        w_hi = {n: sem(f"w{n}_hi_ready") for n in "qkvo"}
        w_lo = {n: sem(f"w{n}_lo_ready") for n in "qkvo"}
        x_loaded = sem("x_loaded")
        c_loaded = sem("c_loaded")
        stats_done = sem("stats_done")
        stats_seen = sem("stats_seen")
        mv_done = sem("mv_done")
        lnv_done = sem("lnv_done")
        rstd_done = sem("rstd_done")
        xn_ready = sem("xn_ready")
        xt_done = sem("xt_done")
        xnT_hi_ready = sem("xnT_hi_ready")
        xnT_lo_ready = sem("xnT_lo_ready")
        cT_hi_ready = sem("cT_hi_ready")
        cT_lo_ready = sem("cT_lo_ready")
        proj_done = sem("proj_done")
        proj_hi_staged = sem("proj_hi_staged")
        proj_taken = sem("proj_taken")
        stored = {n: [sem(f"stored_{n}{s}") for s in range(2)] for n in "qkv"}
        prep_done = sem("prep_done")
        prep_hi = sem("prep_hi")
        prep_taken = sem("prep_taken")

        qk_loaded = [sem(f"qk_loaded{c}") for c in range(GB)]
        v_loaded = [sem(f"v_loaded{c}") for c in range(GB)]
        ones_row_set = sem("ones_row_set")
        pass_a_done = sem("pass_a_done")
        max_taken = sem("max_taken")
        max_transposed = sem("max_transposed")
        negmax_ready = sem("negmax_ready")
        maxrow_loaded = sem("maxrow_loaded")
        pass_b_done = sem("pass_b_done")
        exp_done = sem("exp_done")
        pv_done = sem("pv_done")
        pair_ready = sem("pair_ready")
        sum_ready = sem("sum_ready")
        den_done = sem("den_done")
        lnden_done = sem("lnden_done")
        invden_ready = sem("invden_ready")
        attn_taken = sem("attn_taken")
        aT_hi_ready = sem("aT_hi_ready")
        aT_lo_ready = sem("aT_lo_ready")
        res_loaded = [sem(f"res_loaded{t}") for t in range(NT)]
        res_biased = sem("res_biased")
        o_done = sem("o_done")
        x1_ready = sem("x1_ready")
        r_stats_done = sem("r_stats_done")
        r_mv_done = sem("r_mv_done")
        r_lnv_done = sem("r_lnv_done")
        r_rstd_done = sem("r_rstd_done")
        r_shift_done = sem("r_shift_done")
        rn_ready = sem("rn_ready")
        x1_biased = sem("x1_biased")
        rt_done = sem("rt_done")
        rnT_hi_ready = sem("rnT_hi_ready")
        rnT_lo_ready = sem("rnT_lo_ready")
        z_done = sem("z_done")
        z_taken = sem("z_taken")
        sig_step = sem("sig_step")
        gates_ready = sem("gates_ready")
        tree_step = sem("tree_step")
        lt_done = sem("lt_done")
        lpT_hi_ready = sem("lpT_hi_ready")
        lpT_lo_ready = sem("lpT_lo_ready")
        y_done = sem("y_done")
        out_ready = sem("out_ready")
        out_stored = [sem(f"out_stored{t}") for t in range(NT)]

        PROJ_FREE, STAGE_FREE = 6, 32
        RING = 2
        NPROJ = 3 * KC
        PAIRS = NT // 2
        TREE_STEPS = PAIRS * DEPTH
        N_PREP = KC + LC

        A_LEAD = 7
        FOLD_UNITS = ((), (0,), (1,), (2,), (3, 4), (5, 6))
        TICKS = GB * NT

        SIDE = {
            0: [("y", 2, 0), ("lt", 2, 1)],
            1: [("max", 0, 0), ("y", 2, 1)],
            2: [("den", 0, 0), ("lt", 2, 2)],
            3: [("y", 2, 2), ("lt", 2, 3)],
            4: [("y", 2, 3)],
            5: [("max", 0, 1), ("o", 1, 0)],
            6: [("den", 0, 1), ("o", 1, 1)],
            7: [("o", 1, 2)],
            8: [("o", 1, 3)],
            9: [("max", 0, 2)],
            10: [("den", 0, 2), ("rt", 1, 0)],
            11: [("z", 1, 0), ("rt", 1, 1)],
            12: [("z", 1, 1), ("rt", 1, 2)],
            13: [("max", 0, 3), ("z", 1, 2), ("rt", 1, 3)],
            14: [("den", 0, 3), ("z", 1, 3)],
            15: [("lt", 1, 0)],
        }
        RSTD_AT, RN_TICK = {9: 0, 10: 1}, 10
        RSTD_TILES = (slice(0, 3), slice(3, 4))
        SIGMOID_AT = {(13, 2): (1, 0, 0), (13, 4): (1, 0, 1), (14, 0): (1, 0, 2), (14, 1): (1, 0, 3),
                      (15, 2): (1, 1, 0), (15, 3): (1, 1, 1), (0, 0): (2, 1, 2), (0, 1): (2, 1, 3)}
        TREE_AT = {(14, 2): (1, 0, (0, 1, 2, 3)), (14, 3): (1, 0, (4, 5, 6, 7)),
                   (0, 2): (2, 1, (0, 1, 2, 3)), (0, 3): (2, 1, (4, 5)), (1, 2): (2, 1, (6,)), (1, 3): (2, 1, (7,))}
        TAKE_SLOT = {"rt": 1, "lt": 1, "o": 1, "z": 0, "y": 1, "max": None, "den": None}
        HI_ATTN_AT = ((1, 2), (5, 0), (9, 2), (13, 2))
        LO_ATTN_AT = ((2, 1), (5, 1), (10, 1), (14, 1))

        def side_at(tick, back, has_next):
            found = []
            for kind, ago, n in SIDE.get(tick, []):
                if kind == "max" and n == GB - 1 and not has_next:
                    continue
                if kind == "den" and n == 0 and not back:
                    continue
                if ago <= back:
                    found.append((kind, ago, n))
            return found

        class Turns:

            def __init__(self):
                self.next = 0
                self.where = {}

            def take(self, kind, tile=0):
                self.where[kind, tile] = bank_g[self.next]
                self.next = 1 - self.next
                return self.where[kind, tile]

        def pass_a_unit(b, u, has_next):
            v = u + A_LEAD
            if not has_next and v >= TICKS:
                return None
            return b + v // TICKS, v % TICKS // NT, v % NT

        def term_pairs():
            return ((0, 0), (0, 1), (1, 0))

        def stacks_free(eng):
            eng.wait_ge(proj_taken, PROJ_FREE + NPROJ * (B - 1) + 2 * KC)

        def phase0_over(eng):
            eng.wait_ge(proj_taken, PROJ_FREE + NPROJ * B)
            eng.wait_ge(prep_taken, N_PREP)
            eng.wait_ge(cT_lo_ready, KC * B)
            for s in range(2):
                for n in "qkv":
                    per = 16 if n == "v" else 32
                    eng.wait_ge(stored[n][s], STAGE_FREE + per * 2 * B)

        block = ctx.enter_context(nc.Block())

        @block.sync
        def _(sp):
            for n in "qkv":
                for s in range(2):
                    sp.sem_inc(stored[n][s], STAGE_FREE)
            for n, g in enumerate((g_xattn, g_ffn)):
                sp.dma_start(gates_in[:, n:n + 1], g.partition_broadcast(P)).then_inc(gates_loaded, 16)
            sp.dma_start(x_in[:], x[0].rearrange("(t p) d -> p t d", p=P)).then_inc(x_loaded, 16)
            sp.dma_start(ident[:], ident_in).then_inc(ident_loaded, 16)
            for n, (w, s) in enumerate(((WqT, w_loaded[0]), (WkT, w_loaded[1]), (WvT, w_loaded[2]))):
                sp.dma_start(raw[:, n, :].rearrange("p (k e) -> p k e", k=KC),
                             w.rearrange("(k p) e -> p k e", p=P)).then_inc(s, 16)
                if n == 0:
                    sp.dma_start(c_in[:], ctxT[0].rearrange("(k p) s -> p k s", p=P)).then_inc(c_loaded, 16)
            sp.dma_start(b_q[:], bq).then_inc(small_loaded, 16)
            sp.dma_start(b_k[:], bk).then_inc(small_loaded, 16)
            for dst, src in ((b_v, bv), (g_bo, bo), (g_wb, Wout_b)):
                sp.dma_start(dst[:], src.partition_broadcast(P)).then_inc(small_loaded, 16)
            def load_stacks(b, c, which="qk"):
                for n, stack, dram, parts in (("q", q_stack, qT_dram, (0, 0, 1)), ("k", k_stack, kT_dram, (0, 1, 0))):
                    if n in which:
                        for r, part in enumerate(parts):
                            sp.dma_start(stack[DH * r:DH * (r + 1), c, :, :].bitcast(F32), dram[b, c, part]
                                         ).then_inc(qk_loaded[c], 16)

            def load_v(b, c):
                sp.dma_start(v_sb[:, c, :, :], v_dram[b, c]).then_inc(v_loaded[c], 16)

            def load_x(b):
                sp.wait_ge(xn_ready, NT * b)
                sp.dma_start(x_in[:], x[b].rearrange("(t p) d -> p t d", p=P)).then_inc(x_loaded, 16)

            def batch(b, has_next, has_second):
                if has_next:
                    sp.wait_ge(cT_lo_ready, KC * b + KC)
                    sp.dma_start(c_in[:], ctxT[b + 1].rearrange("(k p) s -> p k s", p=P)).then_inc(c_loaded, 16)
                for n, dram, first in (("q", qT_dram, 0), ("k", kT_dram, KC)):
                    for c in range(GB):
                        sp.wait_ge(proj_taken, PROJ_FREE + NPROJ * b + first + c + 1)
                        for part in range(2):
                            dst = dram[b, c, part].rearrange("d i s -> i d s")
                            sp.dma_start(dst, stage[n][part][:, c % 2, :].bitcast(F32)).then_inc(stored[n][c % 2], 16)
                    if n == "q" and has_second:
                        load_x(b + 2)
                    if n == "q" and not has_next:
                        for s in range(2):
                            for m in "qk":
                                sp.wait_ge(stored[m][s], STAGE_FREE + 64)
                            sp.wait_ge(stored["v"][s], STAGE_FREE + 32)
                        load_stacks(0, 0, "q")
                if not has_next:
                    stacks_free(sp)
                    load_stacks(0, 0, "k")
                for t in range(NT):
                    sp.wait_ge(proj_taken, PROJ_FREE + NPROJ * b + 2 * KC + t + 1)
                    sp.dma_start(v_dram[b, :, :, t, :].rearrange("c p e -> p c e"),
                                 stage_v[:, t % 2, :].rearrange("p (c e) -> p c e", c=GB)
                                 ).then_inc(stored["v"][t % 2], 16)

            load_x(1)
            batch(0, True, True)
            def load_weight(w, dst):
                sp.dma_start(dst.rearrange("p (k e) -> p k e", k=KC)[:, :, 0:w.shape[1]],
                             w.rearrange("(k p) e -> p k e", p=P)).then_inc(ffn_w_loaded, 16)

            sp.wait_ge(raw_cleared, 1)
            load_weight(WoT, raw[:, 0, :])
            with sp.Fori(1, B - 3) as b:
                batch(b, True, True)
            load_weight(ffn_Wq, raw[:, 1, :])
            batch(B - 3, True, True)
            load_weight(WoutT, raw[:, 2, :])
            batch(B - 2, True, False)
            load_weight(leaf_valuesT, raw[:, 3, 0:1024])
            load_weight(routersT, raw[:, 3, 1024:2048])
            batch(B - 1, False, False)


            sp.wait_ge(cT_lo_ready, KC * B)
            for c in range(GB):
                if c:
                    load_stacks(0, c)
                load_v(0, c)
            phase0_over(sp)

            def store_out(b, t):
                sp.wait_ge(out_ready, NT * b + t + 1)
                sp.dma_start(out[b, t * P:(t + 1) * P, :], res[:, t, :]).then_inc(out_stored[t], 16)

            def load_residual(b, t, first=False):
                if not first:
                    sp.wait_ge(out_stored[t], 16 * b)
                sp.dma_start(res[:, t, :], x[b, t * P:(t + 1) * P, :]).then_inc(res_loaded[t], 16)

            def next_group(b, c):
                sp.wait_ge(pv_done, NT + 16 * b + NT * c + NT)
                load_stacks(b + 1, c)
                load_v(b + 1, c)

            def iteration(b, back, has_next):
                for t in range(NT):
                    if back >= 2:
                        store_out(b - 2, t)
                    if back >= 1:
                        load_residual(b - 1, t, first=back == 1)
                    if t == 2 and has_next:
                        next_group(b, 0)
                if has_next:
                    for c in range(1, GB):
                        next_group(b, c)

            iteration(0, 0, True)
            iteration(1, 1, True)
            with sp.Fori(2, B - 1) as b:
                iteration(b, 2, True)
            iteration(B - 1, 2, False)
            for b in (B - 2, B - 1):
                for t in range(NT):
                    store_out(b, t)
                    if b == B - 2:
                        load_residual(B - 1, t)
            for t in range(NT):
                sp.wait_ge(out_stored[t], 16 * B)

        @block.tensor
        def _(pe):
            def transposes(dst, src_of, n):
                for m in range(n):
                    last = nc.tensor.transpose(dst[:, m * P:(m + 1) * P], src_of(m), ident[:])
                return last

            def split_matmul(dst, left, right, chunks):
                last = None
                for k in range(chunks):
                    for n, (a, m) in enumerate(term_pairs()):
                        last = nc.tensor.matmul(dst, left(a, k), right(m, k), start=(k == 0 and n == 0),
                                                stop=(k == chunks - 1 and n == 2))
                return last

            def transpose_xn(b, k, first=False):
                if not (first and k < 2):
                    pe.wait_ge(xnT_lo_ready, KC * b + k - 1)
                transposes(bank[6 + k % 2], lambda t: xn[:, t, k * P:(k + 1) * P], NT).then_inc(xt_done, 1)

            pe.wait_ge(ident_loaded, 16)
            pe.wait_ge(xn_ready, NT)
            for k in range(KC):
                transpose_xn(0, k, first=True)

            fq = raw[:, 1, :].rearrange("p (k e) -> p k e", k=KC)
            fo = raw[:, 2, :].rearrange("p (k e) -> p k e", k=KC)
            lv = raw[:, 3, 0:1024].rearrange("p (k e) -> p k e", k=KC)
            ro = raw[:, 3, 1024:2048].rearrange("p (k e) -> p k e", k=KC)

            def score_a(b, c, i, t):
                n = GB * 16 * b + 16 * c + 4 * i + t
                if isinstance(n, int) and n == 0:
                    stacks_free(pe)
                if i == 0 and t == 0:
                    pe.wait_ge(qk_loaded[c], 96 * b + 96)
                pe.wait_ge(max_taken, n + 1)
                nc.tensor.matmul(bank_a[t % 2][:], q_stack[0:STACK, c, i, t * P:(t + 1) * P],
                                 k_stack[0:STACK, c, i, :], start=True, stop=True).then_inc(pass_a_done, 1)

            def fold_weights(n):
                tiles = [(u, t) for u in FOLD_UNITS[n] for t in range(NT)]
                dst = bank[6 + n % 2]
                if n == 0:
                    pe.wait_ge(ffn_w_loaded, 16 * 5)
                    pe.wait_ge(xnT_lo_ready, KC * B)
                if n >= 2:
                    pe.wait_ge(prep_taken, n - 1)
                for k in range(KC):
                    if n < KC:
                        last = nc.tensor.matmul(dst[:, 0:LEAVES], fq[:, k, n * P:(n + 1) * P], ro[:, k, :],
                                                start=k == 0, stop=k == KC - 1)
                    else:
                        h = n - KC
                        last = nc.tensor.matmul(dst[:], lv[:, k, h * P:(h + 1) * P], fo[:, k, :],
                                                start=k == 0, stop=k == KC - 1)
                    if k == KC - 1:
                        last.then_inc(prep_done, 1)
                    for u, t in tiles[k * len(tiles) // KC:(k + 1) * len(tiles) // KC]:
                        score_a(0, u // HG, u % HG, t)

            def batch(b, has_next, first=False):
                if first:
                    pe.wait_ge(w_lo["q"], 1)
                for c in range(KC):
                    pe.wait_ge(proj_taken, NPROJ * b + c + 1)
                    if c == 0:
                        pe.wait_ge(xnT_lo_ready, KC * b + KC)
                    split_matmul(bank[c][:], lambda a, k: w_in["q"][a][:, k, c * P:(c + 1) * P],
                                 lambda m, k: xnT[m][:, k, :], KC).then_inc(proj_done, 1)
                if first:
                    pe.wait_ge(w_lo["k"], 1)
                for c in range(KC):
                    pe.wait_ge(proj_taken, NPROJ * b + KC + c + 1)
                    if c == 0:
                        pe.wait_ge(cT_lo_ready, KC * b + KC)
                    split_matmul(bank[(KC + c) % 6][:], lambda a, k: w_in["k"][a][:, k, c * P:(c + 1) * P],
                                 lambda m, k: cT[m][:, k, :], KC).then_inc(proj_done, 1)
                    if has_next and c:
                        if c == 1:
                            pe.wait_ge(xn_ready, NT * b + 2 * NT)
                        transpose_xn(b + 1, c - 1)
                if first:
                    pe.wait_ge(w_lo["v"], 1)
                for t in range(NT):
                    pe.wait_ge(proj_taken, NPROJ * b + 2 * KC + t + 1)
                    split_matmul(bank[(2 * KC + t) % 6][:], lambda a, k: cT[a][:, k, t * P:(t + 1) * P],
                                 lambda m, k: w_in["v"][m][:, k, :], KC).then_inc(proj_done, 1)
                    if has_next and t == 1:
                        transpose_xn(b + 1, KC - 1)

            batch(0, True, first=True)
            with pe.Fori(1, B - 1) as b:
                batch(b, True)
            batch(B - 1, False)

            def score_b(b, c, j, i):
                n = GB * 16 * b + 16 * c + 4 * j + i
                if i == 0 and j == 0:
                    pe.wait_ge(maxrow_loaded, 16 * (GB * b + c + 1))
                pe.wait_ge(exp_done, n + 1)
                nc.tensor.matmul(bank_b[i % 2][:], k_stack[0:STACK + 1, c, i, j * P:(j + 1) * P],
                                 q_stack[0:STACK + 1, c, i, :], start=True, stop=True).then_inc(pass_b_done, 1)

            def prob_v(b, c, j):
                g = GB * b + c
                if j == 0:
                    pe.wait_ge(attn_taken, g + 1)
                    pe.wait_ge(v_loaded[c], 16 * b + 16)
                pe.wait_ge(exp_done, RING + 16 * g + 4 * j + 4)
                for i in range(HG):
                    last = nc.tensor.matmul(bank_pv[c % 2][DH * i:DH * (i + 1), :],
                                            v_sb[:, c, j, DH * i:DH * (i + 1)],
                                            prob[:, j, i * S:(i + 1) * S], start=j == 0, stop=j == NT - 1)
                last.then_inc(pv_done, 1)

            turns = Turns()
            readers = [[], []]

            def take_bank(kind, tile, *reader):
                s = turns.next
                for sema, value in readers[s]:
                    pe.wait_ge(sema, value)
                readers[s] = [reader]
                return turns.take(kind, tile)

            def transpose_max(b, c):
                g = GB * b + c
                dst = take_bank("max", c, negmax_ready, g + 1)
                pe.wait_ge(max_taken, RING + 16 * g + 16)
                nc.tensor.transpose(dst[0:HG * NT, 0:P], rowmax[:, c % 2, :], ident[:]).then_inc(max_transposed, 1)

            def denominators(b, c, dst=None, pairs=(1,)):
                g = GB * b + c
                if dst is None:
                    dst = take_bank("den", c, lnden_done, g + 1)
                if len(pairs) == 1:
                    pe.wait_ge(sum_ready, g + 1)
                else:
                    pe.wait_ge(pair_ready, 2 + 2 * g + 2)
                for h in pairs:
                    for i in range(HG):
                        last = nc.tensor.matmul(dst[DH * i:DH * (i + 1), :], ones[:],
                                                pair_sum[:, h, i * S:(i + 1) * S],
                                                start=h == pairs[0], stop=h == pairs[-1])
                last.then_inc(den_done, 1)

            def project_out(b, t):
                dst = take_bank("o", t, x1_ready, NT * b + t + 1)
                pe.wait_ge(aT_lo_ready, GB * b + GB)
                split_matmul(dst[:], lambda a, k: aT[a][:, k, t * P:(t + 1) * P],
                             lambda m, k: wo[m][:, k, :], KC).then_inc(o_done, 1)

            def transpose_rn(b, t):
                dst = take_bank("rt", t, rnT_lo_ready, NT * b + t + 1)
                pe.wait_ge(rn_ready, NT * b + t + 1)
                transposes(dst, lambda k: rn[:, k * P:(k + 1) * P], KC).then_inc(rt_done, 1)

            def route(b, t):
                dst = take_bank("z", t, z_taken, NT * b + t + 1)
                pe.wait_ge(rnT_lo_ready, NT * b + t + 1)
                split_matmul(dst[:, 0:LEAVES], lambda a, k: rnT[a][:, k, :],
                             lambda m, k: wz[m][:, k, :], KC).then_inc(z_done, 1)

            def transpose_lp(b, t):
                dst = take_bank("lt", t, lpT_lo_ready, NT * b + t + 1)
                pe.wait_ge(tree_step, TREE_STEPS * b + DEPTH * (t // 2 + 1))
                transposes(dst, lambda h: lp[:, t, h * P:(h + 1) * P], LC).then_inc(lt_done, 1)

            def leaf_out(b, t, dst=None):
                if dst is None:
                    dst = take_bank("y", t, out_ready, NT * b + t + 1)
                pe.wait_ge(lpT_lo_ready, NT * b + t + 1)
                split_matmul(dst[:], lambda a, k: lpT[a][:, k, :], lambda m, k: wy[m][:, k, :], LC).then_inc(y_done, 1)

            side_jobs = {"o": project_out, "rt": transpose_rn, "z": route, "lt": transpose_lp, "y": leaf_out}

            def group_of(b, u):
                return b + u // TICKS, u % TICKS // NT

            def tick(b, u, back, has_next):
                c, j = u // NT, u % NT
                ahead = pass_a_unit(b, u, has_next)
                for i in range(HG):
                    score_b(b, c, j, i)
                    if ahead:
                        score_a(*ahead, i)
                    if i == 1 and (u or back):
                        prob_v(*group_of(b, u - 1), (j - 1) % NT)
                for kind, ago, n in side_at(u, back, has_next):
                    if kind == "max":
                        transpose_max(*group_of(b, NT * (n + 1)))
                    elif kind == "den":
                        denominators(*group_of(b, NT * (n - 1)))
                    else:
                        side_jobs[kind](b - ago, n)

            def iteration(b, back, has_next):
                known = [(negmax_ready, GB * b + 1)]
                if back:
                    known.append((lnden_done, GB * b - 1))
                    if back > 1:
                        known.append((z_taken, NT * (b - 1)))
                        known.append((lpT_lo_ready, NT * (b - 2) + 1))
                turns.next = 0
                readers[0], readers[1] = list(known), list(known)
                for u in range(TICKS):
                    tick(b, u, back, has_next)

            for n in range(N_PREP):
                fold_weights(n)
                if n == 4:
                    pe.wait_ge(max_taken, RING + 16)
                    nc.tensor.transpose(bank[2][0:HG * NT, 0:P], rowmax[:, 0, :], ident[:]).then_inc(max_transposed, 1)
            pe.wait_ge(ones_row_set, GB)
            pe.wait_ge(prep_taken, N_PREP)
            phase0_over(pe)
            iteration(0, 0, True)
            iteration(1, 1, True)
            with pe.Fori(2, B - 1) as b:
                iteration(b, 2, True)
            iteration(B - 1, 2, False)

            last = B - 1
            prob_v(last, GB - 1, NT - 1)
            pe.wait_ge(lnden_done, GB * B - 1)
            pe.wait_ge(z_taken, NT * last)

            def end_transpose_lp(b, t, dst):
                pe.wait_ge(tree_step, TREE_STEPS * b + DEPTH * (t // 2 + 1))
                transposes(dst, lambda h: lp[:, t, h * P:(h + 1) * P], LC).then_inc(lt_done, 1)

            def end_leaf_out(b, t, dst):
                pe.wait_ge(lpT_lo_ready, NT * b + t + 1)
                split_matmul(dst[:], lambda a, k: end_lpT[a][:, t, k * P:(k + 1) * P],
                             lambda m, k: wy[m][:, k, :], LC).then_inc(y_done, 1)

            end_transpose_lp(last - 1, 1, bank[1])
            leaf_out(last - 1, 0, END_Y_BANK[0])
            end_leaf_out(last - 1, 1, END_Y_BANK[1])
            for t in range(2, NT):
                end_transpose_lp(last - 1, t, bank[t])
            denominators(last, GB - 1, END_DEN_BANK, pairs=(0, 1))
            for t in range(2, NT):
                end_leaf_out(last - 1, t, END_Y_BANK[t])

            def end_project(t):
                if t == 0:
                    pe.wait_ge(aT_lo_ready, GB * B)
                if t == 2:
                    pe.wait_ge(out_ready, NT * last)
                split_matmul(bank[t][:], lambda a, k: aT[a][:, k, t * P:(t + 1) * P],
                             lambda m, k: wo[m][:, k, :], KC).then_inc(o_done, 1)

            def end_transpose_rn(t):
                pe.wait_ge(rn_ready, NT * last + t + 1)
                transposes(bank[4 + t], lambda k: end_rn[:, t, k * P:(k + 1) * P], KC).then_inc(rt_done, 1)

            def end_route(t):
                pe.wait_ge(rnT_lo_ready, NT * last + t + 1)
                split_matmul(bank[t][:, 0:LEAVES], lambda a, k: end_rnT[a][:, t, k * P:(k + 1) * P],
                             lambda m, k: wz[m][:, k, :], KC).then_inc(z_done, 1)

            end_project(0)
            end_project(1)
            end_transpose_rn(0)
            end_project(2)
            end_transpose_rn(1)
            end_route(0)
            end_route(1)
            end_project(3)
            end_transpose_rn(2)
            end_transpose_rn(3)
            end_route(2)
            end_route(3)
            for h in range(PAIRS):
                for t in (2 * h, 2 * h + 1):
                    end_transpose_lp(last, t, bank[4 + t])
                pe.wait_ge(z_taken, NT * last + 2 * h + 2)
                for t in (2 * h, 2 * h + 1):
                    end_leaf_out(last, t, bank[t])

        @block.scalar
        def _(act):
            act.wait_ge(gates_loaded, 32)
            nc.scalar.activation(gain[:], gates_in[:], ACT.Tanh).then_inc(tanh_done, 1)
            nc.scalar.preload_act_table_set("natural_log_exp_and_others")
            act.wait_ge(consts_set, 2)

            def rstd(b):
                act.wait_ge(mv_done, NT * b + NT)
                nc.scalar.activation(x_lnv[:], x_mv[:, :, 1], ACT.Ln, bias=eps[:]).then_inc(lnv_done, 1)
                act.wait_ge(lnv_done, b + 1)
                nc.scalar.activation(x_rstd[:], x_lnv[:], ACT.Exp, scale=-0.5).then_inc(rstd_done, 1)

            def evac_xt(b, k):
                act.wait_ge(xt_done, KC * b + k + 1)
                nc.scalar.copy(xnT[0][:, k, :], bank[6 + k % 2][:]).then_inc(xnT_hi_ready, 1)

            def evac_proj(b, n, c, first):
                act.wait_ge(proj_done, NPROJ * b + first + c + 1)
                act.wait_ge(stored[n][c % 2], STAGE_FREE + 32 * (2 * b + c // 2))
                nc.scalar.activation(stage[n][0][:, c % 2, :], bank[(first + c) % 6][:], ACT.Identity,
                                     bias=(b_q if n == "q" else b_k)[:, c:c + 1]).then_inc(proj_hi_staged, 1)

            def weight_hi(n, slot, dst):
                nc.scalar.copy(dst[0][:].rearrange("p k e -> p (k e)"), raw[:, slot, :]).then_inc(w_hi[n], 1)

            rstd(0)
            act.wait_ge(w_loaded[0], 16)
            weight_hi("q", 0, w_in["q"])
            for k in range(KC):
                evac_xt(0, k)

            def hi_folded(n):
                act.wait_ge(prep_done, n + 1)
                if n < KC:
                    nc.scalar.copy(wz[0][:, n, :], bank[6 + n % 2][:, 0:LEAVES]).then_inc(prep_hi, 1)
                else:
                    nc.scalar.copy(wy[0][:, n - KC, :], bank[6 + n % 2][:]).then_inc(prep_hi, 1)

            def batch(b, has_next, first=False):
                act.wait_ge(c_loaded, 16 * b + 16)
                if not isinstance(b, int) or b:
                    act.wait_ge(proj_done, NPROJ * b)
                for k in range(KC):
                    nc.scalar.copy(cT[0][:, k, :], c_in[:, k, :]).then_inc(cT_hi_ready, 1)
                if first:
                    for slot, n in ((1, "k"), (2, "v")):
                        act.wait_ge(w_loaded[slot], 16)
                        weight_hi(n, slot, w_in[n])
                    act.wait_ge(small_loaded, 16 * 5)
                if has_next and not first:
                    rstd(b + 1)
                if not has_next:
                    act.wait_ge(ffn_w_loaded, 16 * 5)
                    weight_hi("o", 0, wo)
                for c in range(KC):
                    evac_proj(b, "q", c, 0)
                    if first and c == 2:
                        rstd(b + 1)
                for c in range(KC):
                    evac_proj(b, "k", c, KC)
                    if has_next and c:
                        evac_xt(b + 1, c - 1)
                if has_next:
                    evac_xt(b + 1, KC - 1)

            batch(0, True, first=True)
            with act.Fori(1, B - 1) as b:
                batch(b, True)
            batch(B - 1, False)

            def row_of_maxima(b, c, src, first=False):
                g = GB * b + c
                act.wait_ge(max_transposed, g + 1)
                if not first:
                    act.wait_ge(maxrow_loaded, 16 * g)
                nc.scalar.mul(negmax[:], src[0:HG * NT, 0:P], -1.0).then_inc(negmax_ready, 1)
                act.wait_ge(negmax_ready, g + 1)
                act.dma_start(q_stack[STACK:STACK + 1, c, :, :].rearrange("o i (t q) -> o (i t) q", q=P).bitcast(F32),
                              negmax[:].bitcast(F32)).then_inc(maxrow_loaded, 16)

            for n in range(N_PREP):
                hi_folded(n)
                if n == 4:
                    row_of_maxima(0, 0, bank[2], first=True)

            turns = Turns()

            def exp_scores(b, c, j, i):
                g = GB * b + c
                n = 16 * g + 4 * j + i
                act.wait_ge(pass_b_done, n + 1)
                if i == 0:
                    act.wait_ge(pv_done, 4 * g + j + 1)
                    act.wait_ge(pair_ready, 2 * g + j // 2 + 1)
                nc.scalar.activation(prob[:, j, i * S:(i + 1) * S], bank_b[i % 2][:], ACT.Exp,
                                     scale=SCALE).then_inc(exp_done, 1)

            def invert_denominators(b, c, src):
                g = GB * b + c
                act.wait_ge(den_done, 1 + g + 1)
                act.wait_ge(attn_taken, RING + g)
                nc.scalar.activation(inv_den[:], src[:], ACT.Ln).then_inc(lnden_done, 1)
                act.wait_ge(lnden_done, g + 1)
                nc.scalar.activation(inv_den[:], inv_den[:], ACT.Exp, scale=-1.0).then_inc(invden_ready, 1)

            def hi_attn(b, c):
                act.wait_ge(attn_taken, RING + GB * b + c + 1)
                if not isinstance(b, int) or b:
                    act.wait_ge(o_done, NT * b)
                nc.scalar.copy(aT[0][:, c, :], attn[:]).then_inc(aT_hi_ready, 1)

            def rstd1(b, part, t=None):
                tiles, n = (RSTD_TILES[part], 2 * b + part) if t is None else (slice(t, t + 1), 2 * b + t)
                act.wait_ge(r_mv_done, NT * b + tiles.stop)
                nc.scalar.activation(r_lnv[:, tiles], r_mv[:, tiles, 1], ACT.Ln, bias=eps[:]).then_inc(r_lnv_done, 1)
                act.wait_ge(r_lnv_done, n + 1)
                nc.scalar.activation(r_rstd[:, tiles], r_lnv[:, tiles], ACT.Exp, scale=-0.5).then_inc(r_rstd_done, 1)

            def normalise1(b, t, dst):
                n = NT * b + t
                act.wait_ge(r_shift_done, 2 * b + (1 + t // 3 if dst is rn else t + 1))
                if dst is rn and (not isinstance(b, int) or n):
                    act.wait_ge(rt_done, n)
                nc.scalar.activation(dst[:], res[:, t, :], ACT.Identity, bias=r_shift[:, t:t + 1],
                                     scale=r_rstd[:, t:t + 1]).then_inc(rn_ready, 1)

            def evac_rt(b, t, src, dst, shared=True):
                n = NT * b + t
                act.wait_ge(rt_done, n + 1)
                if shared:
                    act.wait_ge(z_done, 1 + n)
                nc.scalar.copy(dst, src[:]).then_inc(rnT_hi_ready, 1)

            def sigmoid(b, h, step):
                n = PAIRS * b + h
                tiles = gate[:, 2 * h:2 * h + 2, :]
                if step == 0:
                    act.wait_ge(z_taken, 2 * n + 2)
                else:
                    act.wait_ge(sig_step, 3 * n + step)
                if step == 0:
                    nc.scalar.activation(tiles, tiles, ACT.Exp, scale=-1.0).then_inc(sig_step, 1)
                elif step == 1:
                    nc.scalar.activation(tiles, tiles, ACT.Ln, bias=one_col).then_inc(sig_step, 1)
                elif step == 2:
                    nc.scalar.activation(tiles, tiles, ACT.Exp, scale=-1.0).then_inc(sig_step, 1)
                else:
                    nc.scalar.activation(ungate[:, 2 * h:2 * h + 2, :], tiles, ACT.Identity, bias=one_col,
                                         scale=-1.0).then_inc(gates_ready, 1)

            def evac_lt(b, t, src, dst):
                n = NT * b + t
                act.wait_ge(lt_done, n + 1)
                if dst is lpT[0]:
                    act.wait_ge(y_done, 1 + n)
                    dst = dst[:].rearrange("p k q -> p (k q)")
                nc.scalar.copy(dst, src[:, 0:LC * P]).then_inc(lpT_hi_ready, 1)

            one_col = ones[:, 0:1]

            def group_of(b, u):
                return b + u // TICKS, u % TICKS // NT

            def side_work(b, entries):
                for kind, ago, t in entries:
                    if kind == "rt":
                        evac_rt(b - ago, t, turns.where["rt", t], rnT[0][:].rearrange("p k q -> p (k q)"))
                    if kind == "lt":
                        evac_lt(b - ago, t, turns.where["lt", t], lpT[0])

            def sigmoid_at(b, u, slot, back):
                if (u, slot) in SIGMOID_AT:
                    ago, h, step = SIGMOID_AT[u, slot]
                    if ago <= back:
                        sigmoid(b - ago, h, step)

            def tick(b, u, back, has_next, waiting):
                c, j = u // NT, u % NT
                side_work(*waiting)
                for i in range(HG):
                    exp_scores(b, c, j, i)
                    if (u, i) in HI_ATTN_AT and (c >= 2 or back):
                        hi_attn(*group_of(b, u - 2 * NT))
                    if i == 1 and back and RN_TICK <= u < RN_TICK + NT:
                        normalise1(b - 1, u - RN_TICK, rn)
                    if i == 1 and back and u in RSTD_AT:
                        rstd1(b - 1, RSTD_AT[u])
                    sigmoid_at(b, u, i, back)
                entries = side_at(u, back, has_next)
                for kind, ago, n in entries:
                    src = turns.take(kind, n)
                    if kind == "max":
                        row_of_maxima(*group_of(b, NT * (n + 1)), src)
                    if kind == "den":
                        invert_denominators(*group_of(b, NT * (n - 1)), src)
                sigmoid_at(b, u, NT, back)
                return b, entries

            def iteration(b, back, has_next):
                turns.next = 0
                waiting = (b, [])
                for u in range(TICKS):
                    waiting = tick(b, u, back, has_next, waiting)
                side_work(*waiting)

            phase0_over(act)
            act.wait_ge(w_lo["o"], 1)
            iteration(0, 0, True)
            iteration(1, 1, True)
            with act.Fori(2, B - 1) as b:
                iteration(b, 2, True)
            iteration(B - 1, 2, False)

            last = B - 1

            def end_evac_lp(b, t, src):
                if b == last:
                    act.wait_ge(y_done, 1 + NT * last)
                evac_lt(b, t, src, end_lpT[0][:, t, 0:LC * P])

            for step in range(2, 4):
                sigmoid(last - 1, 1, step)
            end_evac_lp(last - 1, 1, bank[1])
            hi_attn(last, GB - 2)
            for t in range(2, NT):
                end_evac_lp(last - 1, t, bank[t])
            invert_denominators(last, GB - 1, END_DEN_BANK)
            hi_attn(last, GB - 1)

            def end_normalise(t):
                rstd1(last, None, t)
                normalise1(last, t, end_rn[:, t, :])

            def end_evac_rt(t):
                evac_rt(last, t, bank[4 + t], end_rnT[0][:, t, :], shared=False)

            end_normalise(0)
            end_evac_rt(0)
            end_normalise(1)
            end_evac_rt(1)
            end_normalise(2)
            for step in range(4):
                sigmoid(last, 0, step)
            end_evac_rt(2)
            end_normalise(3)
            end_evac_rt(3)
            sigmoid(last, 1, 0)
            end_evac_lp(last, 0, bank[4])
            end_evac_lp(last, 1, bank[5])
            for step in range(1, 4):
                sigmoid(last, 1, step)
            end_evac_lp(last, 2, bank[6])
            end_evac_lp(last, 3, bank[7])

        @block.vector
        def _(dve):
            nc.vector.memset(ones[:], 1.0).then_inc(consts_set, 1)
            nc.vector.memset(eps[:], LN_EPS).then_inc(consts_set, 1)
            dve.sem_inc(proj_taken, PROJ_FREE)
            dve.sem_inc(max_taken, RING)
            dve.sem_inc(attn_taken, RING)

            def statistics(b):
                dve.wait_ge(x_loaded, 16 * b + 16)
                for t in range(NT):
                    nc.vector.bn_stats(x_stats[:, t, :], x_in[:, t, :]).then_inc(stats_done, 1)
                dve.wait_ge(stats_done, NT * b + NT)
                dve.sem_inc(stats_seen, 1)
                for t in range(NT):
                    nc.vector.bn_aggr(x_mv[:, t, :], x_stats[:, t, :]).then_inc(mv_done, 1)

            def normalise(b, first=False):
                dve.wait_ge(rstd_done, b + 1)
                if not first:
                    dve.wait_ge(xt_done, KC * b)
                for t in range(NT):
                    nc.vector.tensor_scalar(xn[:, t, :], x_in[:, t, :], x_mv[:, t, 0:1], x_rstd[:, t:t + 1],
                                            ALU.subtract, ALU.mult).then_inc(xn_ready, 1)

            def lo_xt(b, k):
                dve.wait_ge(xnT_hi_ready, KC * b + k + 1)
                nc.vector.tensor_tensor(xnT[1][:, k, :], bank[6 + k % 2][:], xnT[0][:, k, :].bitcast(F32),
                                        ALU.subtract).then_inc(xnT_lo_ready, 1)

            statistics(0)
            normalise(0, first=True)
            for k in range(KC):
                lo_xt(0, k)

            def lo_proj(b, n, c, first):
                done = (NPROJ - NT) * b + first + c + 1
                dve.wait_ge(proj_hi_staged, done)
                nc.vector.scalar_tensor_tensor(
                    out=stage[n][1][:, c % 2, :], in0=bank[(first + c) % 6][:],
                    scalar=(b_q if n == "q" else b_k)[:, c:c + 1], in1=stage[n][0][:, c % 2, :].bitcast(F32),
                    op0=ALU.add, op1=ALU.subtract).then_inc(proj_taken, 1)

            def lo_folded(n):
                dve.wait_ge(prep_hi, n + 1)
                if n < KC:
                    hi, lo, src = wz[0][:, n, :], wz[1][:, n, :], bank[6 + n % 2][:, 0:LEAVES]
                else:
                    hi, lo, src = wy[0][:, n - KC, :], wy[1][:, n - KC, :], bank[6 + n % 2][:]
                nc.vector.tensor_tensor(lo, src, hi.bitcast(F32), ALU.subtract).then_inc(prep_taken, 1)

            def row_max(b, c, i, t):
                n = GB * 16 * b + 16 * c + 4 * i + t
                dve.wait_ge(pass_a_done, n + 1)
                nc.vector.reduce_max(rowmax[:, c % 2, 4 * i + t:4 * i + t + 1], bank_a[t % 2][:], AX_X
                                     ).then_inc(max_taken, 1)

            def batch(b, has_next, first=False):
                if not has_next:
                    dve.wait_ge(w_hi["o"], 1)
                    nc.vector.tensor_tensor(wo[1][:].rearrange("p k e -> p (k e)"), raw[:, 0, :],
                                            wo[0][:].rearrange("p k e -> p (k e)").bitcast(F32),
                                            ALU.subtract).then_inc(w_lo["o"], 1)
                if has_next and not first:
                    statistics(b + 1)
                for c in range(KC):
                    lo_proj(b, "q", c, 0)
                    if first and c == 1:
                        statistics(b + 1)
                    if has_next and c == (3 if first else 1):
                        normalise(b + 1)
                for c in range(KC):
                    lo_proj(b, "k", c, KC)
                    if has_next and c:
                        lo_xt(b + 1, c - 1)
                if first:
                    for n in "qkv":
                        dve.wait_ge(w_lo[n], 1)
                    nc.vector.memset(raw[:, 3, 1024:2048], 0.0).then_inc(raw_cleared, 1)
                    dve.wait_ge(tanh_done, 1)
                    nc.vector.tensor_scalar(g_bo[:], g_bo[:], gain[:, 0:1], None, ALU.mult).then_inc(consts_set, 1)
                    nc.vector.tensor_scalar(g_wb[:], g_wb[:], gain[:, 1:2], None, ALU.mult).then_inc(consts_set, 1)
                for t in range(NT):
                    if has_next and t == 2:
                        lo_xt(b + 1, KC - 1)
                    dve.wait_ge(proj_done, NPROJ * b + 2 * KC + t + 1)
                    dve.wait_ge(stored["v"][t % 2], STAGE_FREE + 16 * (2 * b + t // 2))
                    nc.vector.tensor_tensor(stage_v[:, t % 2, :], bank[(2 * KC + t) % 6][:], b_v[:],
                                            ALU.add).then_inc(proj_taken, 1)

            dve.wait_ge(w_hi["k"], 1)
            nc.vector.tensor_tensor(w_in["k"][1][:].rearrange("p k e -> p (k e)"), raw[:, 1, :],
                                    w_in["k"][0][:].rearrange("p k e -> p (k e)").bitcast(F32),
                                    ALU.subtract).then_inc(w_lo["k"], 1)
            dve.wait_ge(small_loaded, 16 * 5)
            batch(0, True, first=True)
            with dve.Fori(1, B - 1) as b:
                batch(b, True)
            batch(B - 1, False)

            turns = Turns()

            def normalise_attn(b, c):
                g = GB * b + c
                dve.wait_ge(invden_ready, g + 1)
                if not isinstance(b, int) or g:
                    dve.wait_ge(aT_lo_ready, g)
                nc.vector.tensor_tensor(attn[:], bank_pv[c % 2][:], inv_den[:], ALU.mult).then_inc(attn_taken, 1)

            def lo_attn(b, c):
                dve.wait_ge(aT_hi_ready, GB * b + c + 1)
                nc.vector.tensor_tensor(aT[1][:, c, :], attn[:], aT[0][:, c, :].bitcast(F32),
                                        ALU.subtract).then_inc(aT_lo_ready, 1)

            def add_attn(b, t, src):
                n = NT * b + t
                dve.wait_ge(o_done, n + 1)
                dve.wait_ge(res_biased, n + 1)
                nc.vector.scalar_tensor_tensor(out=res[:, t, :], in0=src[:], scalar=gain[:, 0:1],
                                               in1=res[:, t, :], op0=ALU.mult, op1=ALU.add).then_inc(x1_ready, 1)

            def x1_statistics(b, t):
                n = NT * b + t
                dve.wait_ge(x1_ready, n + 1)
                nc.vector.bn_stats(r_stats[:, t, :], res[:, t, :]).then_inc(r_stats_done, 1)
                dve.wait_ge(r_stats_done, n + 1)
                dve.sem_inc(stats_seen, 1)
                nc.vector.bn_aggr(r_mv[:, t, :], r_stats[:, t, :]).then_inc(r_mv_done, 1)

            def shift(b, part, t=None):
                tiles, n = (RSTD_TILES[part], 2 * b + part) if t is None else (slice(t, t + 1), 2 * b + t)
                dve.wait_ge(r_rstd_done, n + 1)
                nc.vector.scalar_tensor_tensor(out=r_shift[:, tiles], in0=r_mv[:, tiles, 0], scalar=-1.0,
                                               in1=r_rstd[:, tiles], op0=ALU.mult, op1=ALU.mult
                                               ).then_inc(r_shift_done, 1)

            def lo_rt(b, t, src, hi, lo):
                dve.wait_ge(rnT_hi_ready, NT * b + t + 1)
                nc.vector.tensor_tensor(lo, src[:], hi.bitcast(F32), ALU.subtract).then_inc(rnT_lo_ready, 1)

            def take_z(b, t, src):
                n = NT * b + t
                dve.wait_ge(z_done, 1 + n + 1)
                if not isinstance(b, int) or b:
                    dve.wait_ge(tree_step, TREE_STEPS * b)
                nc.vector.tensor_scalar(gate[:, t, :], src[:, 0:LEAVES], Z_FLOOR, None, ALU.max
                                        ).then_inc(z_taken, 1)

            def tree_levels(b, h, levels):
                tiles = slice(2 * h, 2 * h + 2)
                if 0 in levels:
                    dve.wait_ge(gates_ready, PAIRS * b + h + 1)
                    if h == 0 and (not isinstance(b, int) or b):
                        dve.wait_ge(lt_done, NT * b)
                for level in levels:
                    n = 1 << level
                    parents, children = (lp_odd, lp) if (DEPTH - 1 - level) % 2 == 0 else (lp, lp_odd)
                    dst = children[:, tiles, 0:2 * n].rearrange("p t (m two) -> p t m two", two=2)
                    g1 = gate[:, tiles, n - 1:2 * n - 1]
                    g0 = ungate[:, tiles, n - 1:2 * n - 1]
                    if level == 0:
                        nc.vector.tensor_copy(dst[:, :, :, 0], g0)
                        last = nc.vector.tensor_copy(dst[:, :, :, 1], g1)
                    else:
                        dve.wait_ge(tree_step, TREE_STEPS * b + DEPTH * h + level)
                        nc.vector.tensor_tensor(dst[:, :, :, 0], parents[:, tiles, 0:n], g0, ALU.mult)
                        last = nc.vector.tensor_tensor(dst[:, :, :, 1], parents[:, tiles, 0:n], g1, ALU.mult)
                    last.then_inc(tree_step, 1)

            def lo_lt(b, t, src, hi, lo):
                dve.wait_ge(lpT_hi_ready, NT * b + t + 1)
                nc.vector.tensor_tensor(lo, src[:, 0:LC * P], hi.bitcast(F32), ALU.subtract
                                        ).then_inc(lpT_lo_ready, 1)

            def add_ffn(b, t, src):
                n = NT * b + t
                dve.wait_ge(y_done, 1 + n + 1)
                dve.wait_ge(x1_biased, n + 1)
                nc.vector.scalar_tensor_tensor(out=res[:, t, :], in0=src[:], scalar=gain[:, 1:2],
                                               in1=res[:, t, :], op0=ALU.mult, op1=ALU.add).then_inc(out_ready, 1)

            def group_of(b, u):
                return b + u // TICKS, u % TICKS // NT

            def flat(parts, s):
                return parts[s][:].rearrange("p k q -> p (k q)")

            def side_work(b, entries, slot):
                for kind, ago, t in entries:
                    if slot != TAKE_SLOT[kind]:
                        continue
                    src = turns.where[kind, t]
                    if kind == "rt":
                        lo_rt(b - ago, t, src, flat(rnT, 0), flat(rnT, 1))
                    if kind == "lt":
                        lo_lt(b - ago, t, src, flat(lpT, 0), flat(lpT, 1))
                    if kind == "o":
                        add_attn(b - ago, t, src)
                    if kind == "z":
                        take_z(b - ago, t, src)
                    if kind == "y":
                        add_ffn(b - ago, t, src)

            def tick(b, u, back, has_next, waiting):
                c, j = u // NT, u % NT
                ahead = pass_a_unit(b, u, has_next)
                for t in range(NT):
                    if ahead:
                        row_max(*ahead, t)
                    side_work(*waiting, t)
                    if (u, t) in LO_ATTN_AT and (c >= 2 or back):
                        lo_attn(*group_of(b, u - 2 * NT))
                    if t == 3 and j == NT - 1 and (c or back):
                        normalise_attn(*group_of(b, u - NT))
                    if t == 3 and back and u in RSTD_AT:
                        shift(b - 1, RSTD_AT[u])
                    if t == 3:
                        for kind, ago, m in waiting[1]:
                            if kind == "o":
                                x1_statistics(b - ago, m)
                    if (u, t) in TREE_AT:
                        ago, h, levels = TREE_AT[u, t]
                        if ago <= back:
                            tree_levels(b - ago, h, levels)
                entries = side_at(u, back, has_next)
                for kind, ago, n in entries:
                    turns.take(kind, n)
                return b, entries

            def iteration(b, back, has_next):
                turns.next = 0
                waiting = (b, [])
                for u in range(TICKS):
                    waiting = tick(b, u, back, has_next, waiting)
                for slot in range(NT):
                    side_work(*waiting, slot)

            for n in range(N_PREP):
                for u in FOLD_UNITS[n]:
                    for t in range(NT):
                        row_max(0, u // HG, u % HG, t)
                lo_folded(n)
            phase0_over(dve)
            iteration(0, 0, True)
            iteration(1, 1, True)
            with dve.Fori(2, B - 1) as b:
                iteration(b, 2, True)
            iteration(B - 1, 2, False)

            last = B - 1

            def end_lo_lt(b, t, src):
                lo_lt(b, t, src, end_lpT[0][:, t, 0:LC * P], end_lpT[1][:, t, 0:LC * P])

            def end_lo_rt(t):
                lo_rt(last, t, bank[4 + t], end_rnT[0][:, t, :], end_rnT[1][:, t, :])

            def end_add_attn(t):
                add_attn(last, t, bank[t])
                x1_statistics(last, t)

            end_lo_lt(last - 1, 1, bank[1])
            tree_levels(last - 1, 1, range(DEPTH))
            for t in range(2):
                add_ffn(last - 1, t, END_Y_BANK[t])
            lo_attn(last, GB - 2)
            for t in range(2, NT):
                end_lo_lt(last - 1, t, bank[t])
            normalise_attn(last, GB - 1)
            for t in range(2, NT):
                add_ffn(last - 1, t, END_Y_BANK[t])
            lo_attn(last, GB - 1)
            end_add_attn(0)
            shift(last, None, 0)
            end_add_attn(1)
            shift(last, None, 1)
            end_lo_rt(0)
            end_add_attn(2)
            end_lo_rt(1)
            shift(last, None, 2)
            take_z(last, 0, bank[0])
            take_z(last, 1, bank[1])
            end_add_attn(3)
            shift(last, None, 3)
            end_lo_rt(2)
            tree_levels(last, 0, range(6))
            end_lo_rt(3)
            tree_levels(last, 0, (6, 7))
            take_z(last, 2, bank[2])
            take_z(last, 3, bank[3])
            end_lo_lt(last, 0, bank[4])
            end_lo_lt(last, 1, bank[5])
            tree_levels(last, 1, range(DEPTH))
            end_lo_lt(last, 2, bank[6])
            end_lo_lt(last, 3, bank[7])
            for t in range(NT):
                add_ffn(last, t, bank[t])

        @block.gpsimd
        def _(pool):
            def batch(b):
                for k in range(KC):
                    pool.wait_ge(cT_hi_ready, KC * b + k + 1)
                    nc.gpsimd.tensor_tensor(cT[1][:, k, :], c_in[:, k, :], cT[0][:, k, :].bitcast(F32),
                                            ALU.subtract).then_inc(cT_lo_ready, 1)

            def weight_lo(n, slot):
                pool.wait_ge(w_hi[n], 1)
                nc.gpsimd.tensor_tensor(w_in[n][1][:].rearrange("p k e -> p (k e)"), raw[:, slot, :],
                                        w_in[n][0][:].rearrange("p k e -> p (k e)").bitcast(F32),
                                        ALU.subtract).then_inc(w_lo[n], 1)

            weight_lo("q", 0)
            batch(0)
            weight_lo("v", 2)
            with pool.Fori(1, B) as b:
                batch(b)

            stacks_free(pool)
            for c in range(GB):
                nc.gpsimd.memset(k_stack[STACK:STACK + 1, c, :, :].bitcast(F32), 1.0).then_inc(ones_row_set, 1)
            phase0_over(pool)
            pool.sem_inc(exp_done, RING)
            pool.sem_inc(pv_done, NT)
            pool.sem_inc(pair_ready, 2)
            pool.sem_inc(den_done, 1)
            pool.sem_inc(z_done, 1)
            pool.sem_inc(y_done, 1)

            def add_pair(b, c, h):
                g = GB * b + c
                pool.wait_ge(exp_done, RING + 16 * g + 8 * h + 8)
                if h == 1:
                    pool.wait_ge(den_done, g + 1)
                elif not isinstance(b, int) or g:
                    pool.wait_ge(sum_ready, g)
                nc.gpsimd.tensor_tensor(pair_sum[:, h, :], prob[:, 2 * h, :], prob[:, 2 * h + 1, :],
                                        ALU.add).then_inc(pair_ready, 1)

            def add_all(b, c):
                g = GB * b + c
                pool.wait_ge(pair_ready, 2 + 2 * g + 2)
                nc.gpsimd.tensor_tensor(pair_sum[:, 1, :], pair_sum[:, 0, :], pair_sum[:, 1, :],
                                        ALU.add).then_inc(sum_ready, 1)

            def bias_residual(b, t):
                pool.wait_ge(res_loaded[t], 16 * b + 16)
                nc.gpsimd.tensor_tensor(res[:, t, :], res[:, t, :], g_bo[:], ALU.add).then_inc(res_biased, 1)

            def bias_x1(b, t):
                pool.wait_ge(rn_ready, NT * b + t + 1)
                nc.gpsimd.tensor_tensor(res[:, t, :], res[:, t, :], g_wb[:], ALU.add).then_inc(x1_biased, 1)

            def iteration(b, back, has_next):
                for c in range(GB):
                    if back or c:
                        before = (b if c else b - 1, (c - 1) % GB)
                        add_pair(*before, 1)
                        if back and c == 1:
                            bias_residual(b - 1, 0)
                        add_all(*before)
                        if back and c == 1:
                            bias_residual(b - 1, 1)
                    add_pair(b, c, 0)
                    if back and c == 1:
                        bias_residual(b - 1, 2)
                        bias_residual(b - 1, 3)
                if not has_next:
                    add_pair(b, GB - 1, 1)
                if back:
                    for t in range(NT):
                        bias_x1(b - 1, t)

            pool.wait_ge(consts_set, 4)
            iteration(0, 0, True)
            with pool.Fori(1, B - 1) as b:
                iteration(b, 1, True)
            iteration(B - 1, 1, False)
            for t in range(NT):
                bias_residual(B - 1, t)
            for t in range(NT):
                bias_x1(B - 1, t)


def kernel(x, ctx_1024, g_xattn, g_ffn, L0_xattn_Wq, L0_xattn_bq, L0_xattn_Wk, L0_xattn_bk, L0_xattn_Wv,
           L0_xattn_bv, L0_xattn_Wo, L0_xattn_bo, L0_ffn_Wq, L0_ffn_routers, L0_ffn_leaf_keys,
           L0_ffn_leaf_values, L0_ffn_Wout_w, L0_ffn_Wout_b):
    import numpy as _np
    import concourse.bacc as _bacc
    from concourse import mybir as _mybir
    from concourse.bass_utils import run_bass_kernel_spmd as _run

    def laid(a):
        return _np.ascontiguousarray(a)

    def columns(v):
        return _np.asarray(v).reshape(-1, 128).T

    given = {
        "x": x,
        "ctxT": _np.asarray(ctx_1024).transpose(0, 2, 1),
        "g_xattn": g_xattn,
        "g_ffn": g_ffn,
        "WqT": _np.asarray(L0_xattn_Wq).T,
        "bq": columns(L0_xattn_bq),
        "WkT": _np.asarray(L0_xattn_Wk).T,
        "bk": columns(L0_xattn_bk),
        "WvT": _np.asarray(L0_xattn_Wv).T,
        "bv": L0_xattn_bv,
        "WoT": _np.asarray(L0_xattn_Wo).T,
        "bo": L0_xattn_bo,
        "ffn_Wq": L0_ffn_Wq,
        "routersT": _np.asarray(L0_ffn_routers).T,
        "leaf_valuesT": _np.asarray(L0_ffn_leaf_values).T,
        "WoutT": _np.asarray(L0_ffn_Wout_w).T,
        "Wout_b": L0_ffn_Wout_b,
        "ident": _np.eye(128, dtype=_np.float32),
    }
    nc = _bacc.Bacc("TRN2", target_bir_lowering=False, num_devices=1)
    arrays, args = {}, []
    for name, a in given.items():
        a = laid(a)
        arrays[f"in_{name}"] = a
        args.append(nc.dram_tensor(f"in_{name}", a.shape, _mybir.dt.from_np(a.dtype), kind="ExternalInput").ap())
    args.append(nc.dram_tensor("out_x", x.shape, _mybir.dt.float32, kind="ExternalOutput").ap())
    gated_block(nc, *args)
    r = _run(nc, [arrays], core_ids=[0])
    return r.results[0]["out_x"]
```
